# Optimizing a Trainium2 kernel written in Bass

```python
import numpy as np
import jax
import jax.numpy as jnp

def _softmax(x, axis=-1):
    return jax.nn.softmax(x, axis=axis)

def _gelu(x):
    return jax.nn.gelu(x, approximate=True)

def _silu(x):
    return jax.nn.silu(x)

def _sigmoid(x):
    return jax.nn.sigmoid(x)

def _layernorm(x, axis=-1, eps=1e-05):
    m = jnp.mean(x, axis=axis, keepdims=True)
    v = jnp.var(x, axis=axis, keepdims=True)
    return (x - m) / jnp.sqrt(v + eps)

def _scatter_add(tgt, idx, src, axis=0):
    return tgt.at[idx].add(src)

def _segment_sum(src, seg, n):
    return jax.ops.segment_sum(src, seg, n)
kernel_name = 'mk_conv_seq_d2_conv_nchw384_r4_aada41'

def setup_inputs(seed: int=0):
    np.random.seed(seed)
    _w = jnp.asarray

    def _rec_inputs():
        import jax
        import jax.numpy as jnp
        _gk = jax.random.key(seed)
        x = -0.0004039 + 1 * jax.random.normal(jax.random.fold_in(_gk, 1), (32, 96, 32, 32), jnp.float32)
        return x
    x = _rec_inputs()

    def _L0_conv_setup():
        import jax, jax.numpy as jnp
        import numpy as np
        from jax import lax
        DIM = 96
        KEY_DIM = 32
        NUM_HEADS = 8
        MQ = KEY_DIM * NUM_HEADS
        HID = int(DIM * 4.0)
        B, H, W = (32, 32, 32)

        def _p(key, shape, fan_in):
            return jax.random.normal(key, shape, dtype=jnp.float32) * (1.0 / np.sqrt(fan_in))

        def conv1x1_bn(x, w, s, b):
            y = jnp.einsum('bchw,oc->bohw', x, w)
            return y * s[None, :, None, None] + b[None, :, None, None]

        def block_forward(x, wq, sq, bq, wkv, skv, bkv, wp, sp, bp, w1, s1, b1, wdw, bdw, w2, s2, b2):
            b, c, h, w = x.shape
            hw = h * w
            queries = conv1x1_bn(x, wq, sq, bq).reshape(b, NUM_HEADS, KEY_DIM, hw)
            kv = conv1x1_bn(x, wkv, skv, bkv).reshape(b, KEY_DIM, hw)
            key = jax.nn.softmax(kv, axis=2)
            query = jax.nn.softmax(queries, axis=2)
            context = jnp.einsum('bkn,bdn->bkd', key, kv)
            attended = jnp.einsum('bkd,bhkn->bhdn', context, query)
            attended = attended.reshape(b, MQ, h, w)
            attn_out = conv1x1_bn(jax.nn.relu(attended), wp, sp, bp)
            x = x + attn_out
            hdn = conv1x1_bn(x, w1, s1, b1)
            hdn = lax.conv_general_dilated(hdn, wdw, window_strides=(1, 1), padding=((1, 1), (1, 1)), dimension_numbers=('NCHW', 'OIHW', 'NCHW'), feature_group_count=HID) + bdw[None, :, None, None]
            hdn = jax.nn.relu(hdn)
            mlp_out = conv1x1_bn(hdn, w2, s2, b2)
            return x + mlp_out
        key = jax.random.key(seed)
        ks = jax.random.split(key, 20)
        inp = {'x': jax.random.normal(ks[0], (B, DIM, H, W), dtype=jnp.float32), 'key_v_input_reduction': jax.random.normal(ks[1], (B, DIM, H, W), dtype=jnp.float32), 'wq': _p(ks[2], (MQ, DIM), DIM), 'sq': 1.0 + 0.1 * jax.random.normal(ks[3], (MQ,), dtype=jnp.float32), 'bq': 0.1 * jax.random.normal(ks[4], (MQ,), dtype=jnp.float32), 'wkv': _p(ks[5], (KEY_DIM, DIM), DIM), 'skv': 1.0 + 0.1 * jax.random.normal(ks[6], (KEY_DIM,), dtype=jnp.float32), 'bkv': 0.1 * jax.random.normal(ks[7], (KEY_DIM,), dtype=jnp.float32), 'wp': _p(ks[8], (DIM, MQ), MQ), 'sp': 1.0 + 0.1 * jax.random.normal(ks[9], (DIM,), dtype=jnp.float32), 'bp': 0.1 * jax.random.normal(ks[10], (DIM,), dtype=jnp.float32), 'w1': _p(ks[11], (HID, DIM), DIM), 's1': 1.0 + 0.1 * jax.random.normal(ks[12], (HID,), dtype=jnp.float32), 'b1': 0.1 * jax.random.normal(ks[13], (HID,), dtype=jnp.float32), 'wdw': _p(ks[14], (HID, 1, 3, 3), 9), 'bdw': 0.1 * jax.random.normal(ks[15], (HID,), dtype=jnp.float32), 'w2': _p(ks[16], (DIM, HID), HID), 's2': 1.0 + 0.1 * jax.random.normal(ks[17], (DIM,), dtype=jnp.float32), 'b2': 0.1 * jax.random.normal(ks[18], (DIM,), dtype=jnp.float32)}
        return inp
    _L0_conv_all = _L0_conv_setup()
    _L0_conv_in = {k: v for k, v in _L0_conv_all.items() if k in ('key_v_input_reduction', 'wq', 'sq', 'bq', 'wkv', 'skv', 'bkv', 'wp', 'sp', 'bp', 'w1', 's1', 'b1', 'wdw', 'bdw', 'w2', 's2', 'b2')}
    del _L0_conv_all

    def _L1_conv_setup():
        import jax, jax.numpy as jnp
        import numpy as np
        from jax import lax
        DIM = 96
        HEADS = 6
        K = 3
        PAD = 1
        ITERS = 25
        MLP_HID = 4 * DIM
        EPS = 1e-06
        N, H, W = (32, 28, 28)

        def conv2d(x, w, groups):
            return lax.conv_general_dilated(x, w, window_strides=(1, 1), padding=((PAD, PAD), (PAD, PAD)), dimension_numbers=('NCHW', 'OIHW', 'NCHW'), feature_group_count=groups)

        def transpose_kernel(w, groups):
            co, cig, k, _ = w.shape
            cog = co // groups
            wg = w.reshape(groups, cog, cig, k, k)
            wt = jnp.flip(wg, axis=(3, 4)).transpose(0, 2, 1, 3, 4)
            return wt.reshape(groups * cig, cog, k, k)

        def layernorm_cf(x, g, b):
            mu = x.mean(axis=1, keepdims=True)
            var = ((x - mu) ** 2).mean(axis=1, keepdims=True)
            xn = (x - mu) * lax.rsqrt(var + 1e-06)
            return xn * g[None, :, None, None] + b[None, :, None, None]

        def layernorm_last(x, g, b):
            mu = x.mean(axis=-1, keepdims=True)
            var = ((x - mu) ** 2).mean(axis=-1, keepdims=True)
            return (x - mu) * lax.rsqrt(var + 1e-05) * g + b

        def nnmf_conv(x, w):
            wp = jnp.abs(w)
            wp = wp / jnp.maximum(wp.sum(axis=(1, 2, 3), keepdims=True), EPS)
            wt = transpose_kernel(wp, HEADS)
            x = x / jnp.maximum(x.sum(axis=1, keepdims=True), EPS)
            cout = wp.shape[0]
            h = jnp.full((x.shape[0], cout, x.shape[2], x.shape[3]), 1.0 / cout, x.dtype)

            def step(h, _):
                recon = conv2d(h, wt, HEADS)
                nu = x / jnp.maximum(recon, EPS)
                h = h * conv2d(nu, wp, HEADS)
                h = h / jnp.maximum(h.sum(axis=1, keepdims=True), EPS)
                return (h, None)
            h, _ = lax.scan(step, h, None, length=ITERS)
            return h
        key = jax.random.key(seed)
        ks = jax.random.split(key, 5)
        x = jax.random.normal(ks[0], (N, DIM, H, W), jnp.float32)
        g1 = jnp.ones((DIM,), jnp.float32)
        b1 = jnp.zeros((DIM,), jnp.float32)
        Wc = jax.random.uniform(ks[1], (DIM, DIM // HEADS, K, K), jnp.float32)
        g2 = jnp.ones((DIM,), jnp.float32)
        b2 = jnp.zeros((DIM,), jnp.float32)
        w_fc1 = jax.random.normal(ks[2], (DIM, MLP_HID), jnp.float32) * 0.02
        b_fc1 = jnp.zeros((MLP_HID,), jnp.float32)
        w_fc2 = jax.random.normal(ks[3], (MLP_HID, DIM), jnp.float32) * 0.02
        b_fc2 = jnp.zeros((DIM,), jnp.float32)
        return dict(x=x, g1=g1, b1=b1, Wc=Wc, g2=g2, b2=b2, w_fc1=w_fc1, b_fc1=b_fc1, w_fc2=w_fc2, b_fc2=b_fc2)
    _L1_conv_all = _L1_conv_setup()
    _L1_conv_in = {k: v for k, v in _L1_conv_all.items() if k in ('g1', 'b1', 'Wc', 'g2', 'b2', 'w_fc1', 'b_fc1', 'w_fc2', 'b_fc2')}
    del _L1_conv_all
    return {'x': x, 'L0_conv_key_v_input_reduction': _L0_conv_in['key_v_input_reduction'], 'L0_conv_wq': _L0_conv_in['wq'], 'L0_conv_sq': _L0_conv_in['sq'], 'L0_conv_bq': _L0_conv_in['bq'], 'L0_conv_wkv': _L0_conv_in['wkv'], 'L0_conv_skv': _L0_conv_in['skv'], 'L0_conv_bkv': _L0_conv_in['bkv'], 'L0_conv_wp': _L0_conv_in['wp'], 'L0_conv_sp': _L0_conv_in['sp'], 'L0_conv_bp': _L0_conv_in['bp'], 'L0_conv_w1': _L0_conv_in['w1'], 'L0_conv_s1': _L0_conv_in['s1'], 'L0_conv_b1': _L0_conv_in['b1'], 'L0_conv_wdw': _L0_conv_in['wdw'], 'L0_conv_bdw': _L0_conv_in['bdw'], 'L0_conv_w2': _L0_conv_in['w2'], 'L0_conv_s2': _L0_conv_in['s2'], 'L0_conv_b2': _L0_conv_in['b2'], 'L1_conv_g1': _L1_conv_in['g1'], 'L1_conv_b1': _L1_conv_in['b1'], 'L1_conv_Wc': _L1_conv_in['Wc'], 'L1_conv_g2': _L1_conv_in['g2'], 'L1_conv_b2': _L1_conv_in['b2'], 'L1_conv_w_fc1': _L1_conv_in['w_fc1'], 'L1_conv_b_fc1': _L1_conv_in['b_fc1'], 'L1_conv_w_fc2': _L1_conv_in['w_fc2'], 'L1_conv_b_fc2': _L1_conv_in['b_fc2']}

def reference(x, L0_conv_key_v_input_reduction, L0_conv_wq, L0_conv_sq, L0_conv_bq, L0_conv_wkv, L0_conv_skv, L0_conv_bkv, L0_conv_wp, L0_conv_sp, L0_conv_bp, L0_conv_w1, L0_conv_s1, L0_conv_b1, L0_conv_wdw, L0_conv_bdw, L0_conv_w2, L0_conv_s2, L0_conv_b2, L1_conv_g1, L1_conv_b1, L1_conv_Wc, L1_conv_g2, L1_conv_b2, L1_conv_w_fc1, L1_conv_b_fc1, L1_conv_w_fc2, L1_conv_b_fc2):
    import jax
    import jax.numpy as jnp

    def _L0_conv_ref(x, key_v_input_reduction, wq, sq, bq, wkv, skv, bkv, wp, sp, bp, w1, s1, b1, wdw, bdw, w2, s2, b2):
        import jax, jax.numpy as jnp
        import numpy as np
        from jax import lax
        DIM = 96
        KEY_DIM = 32
        NUM_HEADS = 8
        MQ = KEY_DIM * NUM_HEADS
        HID = int(DIM * 4.0)
        B, H, W = (32, 32, 32)

        def _p(key, shape, fan_in):
            return jax.random.normal(key, shape, dtype=jnp.float32) * (1.0 / np.sqrt(fan_in))

        def conv1x1_bn(x, w, s, b):
            y = jnp.einsum('bchw,oc->bohw', x, w)
            return y * s[None, :, None, None] + b[None, :, None, None]

        def block_forward(x, wq, sq, bq, wkv, skv, bkv, wp, sp, bp, w1, s1, b1, wdw, bdw, w2, s2, b2):
            b, c, h, w = x.shape
            hw = h * w
            queries = conv1x1_bn(x, wq, sq, bq).reshape(b, NUM_HEADS, KEY_DIM, hw)
            kv = conv1x1_bn(x, wkv, skv, bkv).reshape(b, KEY_DIM, hw)
            key = jax.nn.softmax(kv, axis=2)
            query = jax.nn.softmax(queries, axis=2)
            context = jnp.einsum('bkn,bdn->bkd', key, kv)
            attended = jnp.einsum('bkd,bhkn->bhdn', context, query)
            attended = attended.reshape(b, MQ, h, w)
            attn_out = conv1x1_bn(jax.nn.relu(attended), wp, sp, bp)
            x = x + attn_out
            hdn = conv1x1_bn(x, w1, s1, b1)
            hdn = lax.conv_general_dilated(hdn, wdw, window_strides=(1, 1), padding=((1, 1), (1, 1)), dimension_numbers=('NCHW', 'OIHW', 'NCHW'), feature_group_count=HID) + bdw[None, :, None, None]
            hdn = jax.nn.relu(hdn)
            mlp_out = conv1x1_bn(hdn, w2, s2, b2)
            return x + mlp_out
        return block_forward(x, wq, sq, bq, wkv, skv, bkv, wp, sp, bp, w1, s1, b1, wdw, bdw, w2, s2, b2)

    def _L1_conv_ref(x, g1, b1, Wc, g2, b2, w_fc1, b_fc1, w_fc2, b_fc2):
        import jax, jax.numpy as jnp
        import numpy as np
        from jax import lax
        DIM = 96
        HEADS = 6
        K = 3
        PAD = 1
        ITERS = 25
        MLP_HID = 4 * DIM
        EPS = 1e-06
        N, H, W = (32, 28, 28)

        def conv2d(x, w, groups):
            return lax.conv_general_dilated(x, w, window_strides=(1, 1), padding=((PAD, PAD), (PAD, PAD)), dimension_numbers=('NCHW', 'OIHW', 'NCHW'), feature_group_count=groups)

        def transpose_kernel(w, groups):
            co, cig, k, _ = w.shape
            cog = co // groups
            wg = w.reshape(groups, cog, cig, k, k)
            wt = jnp.flip(wg, axis=(3, 4)).transpose(0, 2, 1, 3, 4)
            return wt.reshape(groups * cig, cog, k, k)

        def layernorm_cf(x, g, b):
            mu = x.mean(axis=1, keepdims=True)
            var = ((x - mu) ** 2).mean(axis=1, keepdims=True)
            xn = (x - mu) * lax.rsqrt(var + 1e-06)
            return xn * g[None, :, None, None] + b[None, :, None, None]

        def layernorm_last(x, g, b):
            mu = x.mean(axis=-1, keepdims=True)
            var = ((x - mu) ** 2).mean(axis=-1, keepdims=True)
            return (x - mu) * lax.rsqrt(var + 1e-05) * g + b

        def nnmf_conv(x, w):
            wp = jnp.abs(w)
            wp = wp / jnp.maximum(wp.sum(axis=(1, 2, 3), keepdims=True), EPS)
            wt = transpose_kernel(wp, HEADS)
            x = x / jnp.maximum(x.sum(axis=1, keepdims=True), EPS)
            cout = wp.shape[0]
            h = jnp.full((x.shape[0], cout, x.shape[2], x.shape[3]), 1.0 / cout, x.dtype)

            def step(h, _):
                recon = conv2d(h, wt, HEADS)
                nu = x / jnp.maximum(recon, EPS)
                h = h * conv2d(nu, wp, HEADS)
                h = h / jnp.maximum(h.sum(axis=1, keepdims=True), EPS)
                return (h, None)
            h, _ = lax.scan(step, h, None, length=ITERS)
            return h
        x_norm = layernorm_cf(x, g1, b1)
        x = x + nnmf_conv(jnp.maximum(x_norm, EPS), Wc)
        y = x.transpose(0, 2, 3, 1)
        yn = layernorm_last(y, g2, b2)
        hid = jax.nn.gelu(yn @ w_fc1 + b_fc1, approximate=False)
        y = y + (hid @ w_fc2 + b_fc2)
        return y.transpose(0, 3, 1, 2)

    def _gn(v, G=32, eps=1e-05):
        B_, C_, H_, W_ = v.shape
        g = v.reshape(B_, G, C_ // G, H_, W_)
        m = jnp.mean(g, axis=(2, 3, 4), keepdims=True)
        s = jnp.var(g, axis=(2, 3, 4), keepdims=True)
        return ((g - m) / jnp.sqrt(s + eps)).reshape(v.shape)

    def _ln_c(v, eps=1e-06):
        m = jnp.mean(v, axis=1, keepdims=True)
        s = jnp.var(v, axis=1, keepdims=True)
        return (v - m) / jnp.sqrt(s + eps)

    def _ln_t(v, eps=1e-05):
        m = jnp.mean(v, axis=-1, keepdims=True)
        s = jnp.var(v, axis=-1, keepdims=True)
        return (v - m) / jnp.sqrt(s + eps)

    def _to_tokens(v):
        B_, C_, H_, W_ = v.shape
        return v.reshape(B_, C_, H_ * W_).transpose(0, 2, 1)

    def _from_tokens(t, like):
        B_, C_, H_, W_ = like.shape
        return t.transpose(0, 2, 1).reshape(B_, C_, H_, W_)
    x = _L0_conv_ref(x, L0_conv_key_v_input_reduction, L0_conv_wq, L0_conv_sq, L0_conv_bq, L0_conv_wkv, L0_conv_skv, L0_conv_bkv, L0_conv_wp, L0_conv_sp, L0_conv_bp, L0_conv_w1, L0_conv_s1, L0_conv_b1, L0_conv_wdw, L0_conv_bdw, L0_conv_w2, L0_conv_s2, L0_conv_b2)
    x = _L1_conv_ref(x, L1_conv_g1, L1_conv_b1, L1_conv_Wc, L1_conv_g2, L1_conv_b2, L1_conv_w_fc1, L1_conv_b_fc1, L1_conv_w_fc2, L1_conv_b_fc2)
    return x

_drawn_inputs = setup_inputs


def setup_inputs(seed=0):
    import zlib

    import numpy as np

    out = dict(_drawn_inputs(seed))
    spreads = {'L1_conv_g1': (1.0, 0.6),
     'L1_conv_b1': (0.0, 2.0),
     'L1_conv_g2': (1.0, 0.6),
     'L1_conv_b2': (0.0, 2.0),
     'L1_conv_b_fc1': (0.0, 2.0),
     'L1_conv_b_fc2': (0.0, 0.8)}
    factors = {'L0_conv_sq': 8.0,
     'L0_conv_bq': 8.0,
     'L0_conv_skv': 4.76,
     'L0_conv_sp': 6.088,
     'L1_conv_Wc': 25.888,
     'L0_conv_bp': 8.0,
     'L0_conv_b1': 8.0,
     'L0_conv_bdw': 8.0,
     'L0_conv_b2': 8.0,
     'L1_conv_w_fc1': 8.0,
     'L1_conv_w_fc2': 8.0}
    for name, (base, spread) in spreads.items():
        noise = np.random.default_rng([zlib.crc32(name.encode()), seed]).standard_normal(out[name].shape)
        drawn = base * np.exp(spread * noise) if base else spread * noise
        out[name] = jnp.asarray(drawn.astype(out[name].dtype))
    for name, factor in factors.items():
        out[name] = (out[name] * factor).astype(out[name].dtype)
    return out
```

```python
import numpy as np
from contextlib import ExitStack

import concourse.bass as bass
from concourse import mybir

F32, F16, BF16 = mybir.dt.float32, mybir.dt.float16, mybir.dt.bfloat16
ALU, ACT, AX = mybir.AluOpType, mybir.ActivationFunctionType, mybir.AxisListType

NIMG, CH, HW = 32, 96, 32
GROUPS, GC = 6, 16
PX, PY = 4, 2
AR, AC = HW // PY, HW // PX
BR, BC = AR + 1, AC + 1
CHUNK = 4
A_COLS, B_COLS = CHUNK * AR * AC, CHUNK * BR * BC
ITERS = 25
EPS = 1e-6
H_SCALE, W_SCALE, NU_SCALE = 2.0 ** 14, 2.0 ** 8, 2.0 ** -4
X_SCALE = H_SCALE * W_SCALE * NU_SCALE
NB_A, NB_B = AR * AC, BR * BC


def nnmf(nc, Wc, x_dram, h_dram):
    ctx = ExitStack()
    with ctx:
        sb = lambda n, s, d=F32: ctx.enter_context(nc.sbuf_tensor("nn_" + n, s, d))
        sem = lambda n: ctx.enter_context(nc.semaphore("nn_" + n))
        wraw = sb("wraw", [128, GROUPS, GC, 4, 3])
        wsum = sb("wsum", [128, GROUPS]); wrec = sb("wrec", [128, GROUPS])
        whi = sb("whi", [128, GROUPS, GC, 4, 3], F16); wlo = sb("wlo", [128, GROUPS, GC, 4, 3], F16)
        w1 = sb("w1", [128, 2, 2, 2, GROUPS, 128], F16)
        w2 = sb("w2", [128, 2, 2, 2, GROUPS, 128], F16)
        ident = sb("ident", [128, 128], F16)
        blk = sb("blk", [128, 8, GC])
        hf = [sb(f"hf{u}", [128, GROUPS, A_COLS]) for u in (0, 1)]
        hh = [sb(f"hh{u}", [128, GROUPS, A_COLS], F16) for u in (0, 1)]
        hl = [sb(f"hl{u}", [128, GROUPS, A_COLS], F16) for u in (0, 1)]
        xs = [sb(f"xs{u}", [128, GROUPS, CHUNK, NB_B]) for u in (0, 1)]
        nh = sb("nh", [128, GROUPS, CHUNK, BR, BC], F16)
        nl = sb("nl", [128, GROUPS, CHUNK, BR, BC], F16)
        dd = [sb(f"dd{i}", [128, B_COLS]) for i in range(3)]
        yy = [sb(f"yy{i}", [128, B_COLS]) for i in range(3)]
        ll = [sb(f"ll{i}", [128, B_COLS]) for i in range(2)]
        tt = [sb(f"tt{i}", [128, B_COLS]) for i in range(2)]
        xy = [sb(f"xy{i}", [128, B_COLS]) for i in range(3)]
        nu = [sb(f"nu{i}", [128, B_COLS]) for i in range(3)]
        acc = [sb(f"acc{u}", [128, A_COLS]) for u in (0, 1)]
        sc, sl, sy, stt, sr = (sb(n, [128, A_COLS]) for n in ("sc", "sl", "sy", "st", "sr"))
        P1 = [ctx.enter_context(nc.psum_tensor(f"nn_P1{i}", [128, 2, 512], F32)) for i in range(2)]
        P2 = [ctx.enter_context(nc.psum_tensor(f"nn_P2{i}", [128, 512], F32)) for i in range(3)]
        PS = ctx.enter_context(nc.psum_tensor("nn_PS", [128, 512], F32))
        w_loaded, w_zero, w_abs, w_sum, w_rec, w_norm, w_hi, w_lo = map(sem, ("wld", "wz", "wab", "wsm", "wrc", "wnm", "whi", "wlo"))
        w_max, w_placed, w_turned, w_copied, id_zero, id_done, blk1, blk2, blk_done = map(sem, ("wmx", "wpl", "wtn", "wcp", "idz", "idd", "bk1", "bk2", "bkd"))
        x_loaded = [sem("xl0"), sem("xl1")]
        h_stored = [sem("hs0"), sem("hs1")]
        recon, clamped, logged, inverted, newton, x_over, nu_done, nu_hi, nu_lo = map(sem, ("recon", "clamp", "log", "inv", "newt", "xover", "nu", "nuhi", "nulo"))
        ratio, h_raw, summed, total, s_clamp, s_log, s_inv, s_newt, s_rec = map(sem, ("ratio", "hraw", "summed", "total", "sclamp", "slog", "sinv", "snewt", "srec"))
        h_norm, h_hi, h_lo, h_init = map(sem, ("hnorm", "hhi", "hlo", "hinit"))
        block = ctx.enter_context(nc.Block())
        SLOTS = 2 * ITERS
        PAIRS = NIMG // (2 * CHUNK)
        Pv = [p[:, :, 0:B_COLS // 2] for p in P1]
        half = lambda t: t[:, :].rearrange("p (b n) -> p b n", b=2)

        def PT(q):
            bank = (P1[0][:, 0, :], P1[0][:, 1, :], P1[1][:, 0, :], P1[1][:, 1, :])[q % 4]
            return bank.bitcast(F16)[:, 0:512]

        def schedule(e, slot_fn, last_fn, first_fn):
            with e.Fori(0, PAIRS) as j:
                first_fn(e, j)
                slot_fn(e, j, 0, SLOTS * j, False)
                with e.Fori(0, ITERS - 1) as i:
                    slot_fn(e, j, 1, SLOTS * j + 2 * i + 1, True, (SLOTS - 1) * j + 2 * i + 1)
                    slot_fn(e, j, 0, SLOTS * j + 2 * i + 2, True, (SLOTS - 1) * j + 2 * i + 2)
                slot_fn(e, j, 1, SLOTS * j + 2 * ITERS - 1, True, (2 * ITERS - 1) * j + 2 * ITERS - 1)
                last_fn(e, j)

        @block.sync
        def _(sp):
            sp.wait_ge(w_zero, 1)
            for x in range(PX):
                for y in range(PY):
                    p = 32 * x + 16 * y
                    for g in range(GROUPS):
                        sp.dma_start(wraw[p:p + 16, g, :, y:y + 3, :], Wc[16 * g:16 * g + 16]).then_inc(w_loaded, 16)
            with sp.Fori(0, PAIRS) as j:
                for u in (0, 1):
                    for g in range(GROUPS):
                        sp.dma_start(xs[u][:, g, :, :], x_dram[bass.ds(8 * j + 4 * u, 4), g].rearrange("i p n -> p i n")).then_inc(x_loaded[u], 16)
                for u in (0, 1):
                    sp.wait_ge(h_norm, 6 * SLOTS * j + 6 * SLOTS - 6 * (1 - u))
                    for g in range(GROUPS):
                        sp.dma_start(h_dram[bass.ds(8 * j + 4 * u, 4), g].rearrange("i p n -> p i n"), hf[u][:, g, :].rearrange("p (i n) -> p i n", i=4)).then_inc(h_stored[u], 16)
            for u in (0, 1):
                sp.wait_ge(h_stored[u], 16 * GROUPS * PAIRS)

        @block.gpsimd
        def _(pool):
            pool.memset(ident[:, :], 0.0).then_inc(id_zero, 1)
            pool.wait_ge(id_zero, 1)
            pool.affine_select(out=ident[:, :], in_=ident[:, :], compare_op=ALU.not_equal, fill=1.0, base=0,
                               pattern=[[-1, 128]], channel_multiplier=1).then_inc(id_done, 1)
            pool.memset(blk[:, :, :], 1.0 / H_SCALE).then_inc(blk1, 1)
            pool.wait_ge(blk1, 1)
            pool.affine_select(out=blk[:, :, :], in_=blk[:, :, :], compare_op=ALU.is_ge, fill=0.0, base=0,
                               pattern=[[-GC, 8], [0, GC]], channel_multiplier=1).then_inc(blk2, 1)
            pool.wait_ge(blk2, 1)
            pool.affine_select(out=blk[:, :, :], in_=blk[:, :, :], compare_op=ALU.is_ge, fill=0.0, base=GC - 1,
                               pattern=[[GC, 8], [0, GC]], channel_multiplier=-1).then_inc(blk_done, 1)

            def x_times_inverse(u, k, n):
                pool.wait_ge(inverted, n + k + 1)
                pool.tensor_tensor(xy[k % 3][:, :], xs[u][:, k, :, :].rearrange("p i n -> p (i n)"), yy[k % 3][:, :], ALU.mult).then_inc(x_over, 1)

            def nu_low(k, n):
                pool.wait_ge(nu_hi, n + k + 1)
                pool.tensor_tensor(nl[:, k].rearrange("p i r c -> p (i r c)"), nu[k % 3][:, :],
                                   nh[:, k].rearrange("p i r c -> p (i r c)"), ALU.subtract).then_inc(nu_lo, 1)

            def slot(e, j, u, s, norm, m=0):
                n = 6 * s
                for k in range(6):
                    if norm or k >= 3:
                        e.wait_ge(nu_done, n + k - 2)
                    x_times_inverse(u, k, n)
                    if k >= 2:
                        nu_low(k - 2, n)
                nu_low(4, n)
                nu_low(5, n)
                for k in range(6):
                    e.wait_ge(h_raw, n + k + 1)
                    if k == 1:
                        e.tensor_tensor(acc[u][:, :], hf[u][:, 0, :], hf[u][:, 1, :], ALU.add).then_inc(summed, 1)
                    if k > 1:
                        e.wait_ge(summed, 5 * s + k - 1)
                        e.tensor_tensor(acc[u][:, :], acc[u][:, :], hf[u][:, k, :], ALU.add).then_inc(summed, 1)

            def first(e, j):
                for u in (0, 1):
                    e.wait_ge(x_loaded[u], 96 * j + 96)
            schedule(pool, slot, lambda e, j: None, first)

        @block.scalar
        def _(act):
            act.preload_act_table_set("natural_log_exp_and_others")

            def split(u, k, m):
                act.wait_ge(h_norm, m + k + 1)
                act.activation(hh[u][:, k, :], hf[u][:, k, :], ACT.Copy).then_inc(h_hi, 1)

            def nu_high(k, n, norm):
                act.wait_ge(nu_done, n + k + 1)
                act.activation(nh[:, k].rearrange("p i r c -> p (i r c)"), nu[k % 3][:, :], ACT.Copy).then_inc(nu_hi, 1)

            def slot(e, j, u, s, norm, m=0):
                n = 6 * s
                for k in range(6):
                    e.wait_ge(clamped, n + k + 1)
                    if norm or k >= 2:
                        e.wait_ge(inverted, n + k - 1)
                    e.activation(ll[k % 2][:, :], dd[k % 3][:, :], ACT.Ln).then_inc(logged, 1)
                    e.wait_ge(logged, n + k + 1)
                    if norm or k >= 3:
                        e.wait_ge(x_over, n + k - 2)
                        e.wait_ge(newton, n + k - 2)
                    e.activation(yy[k % 3][:, :], ll[k % 2][:, :], ACT.Exp, scale=-1.0).then_inc(inverted, 1)
                    if norm and k == 3:
                        e.wait_ge(s_clamp, s)
                        e.activation(sl[:, :], sc[:, :], ACT.Ln).then_inc(s_log, 1)
                        e.wait_ge(s_log, s)
                        e.activation(sy[:, :], sl[:, :], ACT.Exp, scale=-1.0).then_inc(s_inv, 1)
                    if k >= 2:
                        nu_high(k - 2, n, norm)
                nu_high(4, n, norm)
                nu_high(5, n, norm)
                if norm:
                    for k in range(6):
                        split(1 - u, k, n - 6)

            def last(e, j):
                s = SLOTS * j + SLOTS
                e.wait_ge(s_clamp, s)
                e.activation(sl[:, :], sc[:, :], ACT.Ln).then_inc(s_log, 1)
                e.wait_ge(s_log, s)
                e.activation(sy[:, :], sl[:, :], ACT.Exp, scale=-1.0).then_inc(s_inv, 1)
            schedule(act, slot, last, lambda e, j: None)

        @block.vector
        def _(dve):
            dve.memset(wraw[:, :, :, :, :], 0.0).then_inc(w_zero, 1)
            dve.memset(w1[:, :, :, :, :, :], 0.0)
            dve.wait_ge(w_loaded, 16 * 48)
            wf = wraw[:, :, :, :, :].rearrange("p g c s x -> p g (c s x)")
            fl = wraw[:, :, :, :, :].rearrange("p g c s x -> p (g c s x)")
            dve.scalar_tensor_tensor(fl, fl, -1.0, fl, ALU.mult, ALU.max).then_inc(w_abs, 1)
            dve.wait_ge(w_abs, 1)
            dve.tensor_reduce(wsum[:, :], wf, AX.X, ALU.add).then_inc(w_sum, 1)
            dve.wait_ge(w_sum, 1)
            dve.tensor_scalar(wsum[:, :], wsum[:, :], EPS, 1.0 / W_SCALE, ALU.max, ALU.mult).then_inc(w_max, 1)
            dve.wait_ge(w_max, 1)
            dve.reciprocal(wrec[:, :], wsum[:, :]).then_inc(w_rec, 1)
            dve.wait_ge(w_rec, 1)
            for g in range(GROUPS):
                dve.tensor_scalar(wf[:, g, :], wf[:, g, :], wrec[:, g:g + 1], None, ALU.mult).then_inc(w_norm, 1)
            dve.wait_ge(w_norm, GROUPS)
            fh, fo = (t[:, :, :, :, :].rearrange("p g c s x -> p (g c s x)") for t in (whi, wlo))
            dve.tensor_copy(fh, fl).then_inc(w_hi, 1)
            dve.wait_ge(w_hi, 1)
            dve.tensor_tensor(fo, fl, fh, ALU.subtract).then_inc(w_lo, 1)
            dve.wait_ge(w_lo, 1)
            for part, src in enumerate((whi, wlo)):
                for b in (0, 1):
                    for xa in range(PX):
                        for xb in range(PX):
                            kx = 2 + xb - 4 * b - xa
                            if 0 <= kx <= 2:
                                q = slice(32 * xa, 32 * xa + 32)
                                for a in (0, 1):
                                    s0 = 2 - 2 * a
                                    dve.tensor_copy(
                                        w1[q, part, a, b, :, :].rearrange("p g (x y c) -> p g x y c", x=4, y=2)[:, :, xb],
                                        src[q, :, :, s0:s0 + 2, kx].rearrange("p g c s -> p g s c")).then_inc(w_placed, 1)
            for q in range(12):
                dve.wait_ge(w_turned, q + 1)
                dve.tensor_copy(w2[:, :, :, :, :, :].rearrange("p h a b g m -> p (h a b g m)")[:, 512 * q:512 * q + 512],
                                PT(q)).then_inc(w_copied, 1)

            def slot(e, j, u, s, norm, m=0):
                n = 6 * s

                def finish_nu(k):
                    e.wait_ge(x_over, n + k + 1)
                    e.wait_ge(newton, n + k + 1)
                    if norm or k >= 3:
                        e.wait_ge(nu_lo, n + k - 2)
                    e.scalar_tensor_tensor(nu[k % 3][:, :], tt[k % 2][:, :], 2.0, xy[k % 3][:, :],
                                           ALU.subtract, ALU.mult, reverse0=True).then_inc(nu_done, 1)

                def residual(k):
                    e.wait_ge(inverted, n + k + 1)
                    if norm or k >= 2:
                        e.wait_ge(nu_done, n + k - 1)
                    e.tensor_tensor(tt[k % 2][:, :], dd[k % 3][:, :], yy[k % 3][:, :], ALU.mult).then_inc(newton, 1)

                for k in range(6):
                    e.wait_ge(recon, n + k + 1)
                    e.tensor_scalar(half(dd[k % 3]), Pv[k % 2], EPS * H_SCALE * W_SCALE, None, ALU.max).then_inc(clamped, 1)
                    if k >= 2:
                        finish_nu(k - 2)
                    if k >= 1:
                        residual(k - 1)
                    if norm and k == 3:
                        e.wait_ge(total, s)
                        e.tensor_scalar(sc[:, :], PS[:, :], EPS * X_SCALE / H_SCALE, None, ALU.max).then_inc(s_clamp, 1)
                    if norm and k == 4:
                        e.wait_ge(s_inv, s)
                        e.tensor_tensor(stt[:, :], sc[:, :], sy[:, :], ALU.mult).then_inc(s_newt, 1)
                    if norm and k == 5:
                        e.wait_ge(s_newt, s)
                        e.scalar_tensor_tensor(sr[:, :], stt[:, :], 2.0, sy[:, :], ALU.subtract, ALU.mult, reverse0=True).then_inc(s_rec, 1)
                finish_nu(4)
                residual(5)
                finish_nu(5)
                o = 1 - u

                def low(k):
                    e.wait_ge(h_hi, 6 * m - 6 + k + 1)
                    e.tensor_tensor(hl[o][:, k, :], hf[o][:, k, :], hh[o][:, k, :], ALU.subtract).then_inc(h_lo, 1)

                for k in range(6):
                    e.wait_ge(ratio, n + k + 1)
                    e.tensor_tensor(hf[u][:, k, :], P2[k % 3][:, :], hf[u][:, k, :], ALU.mult).then_inc(h_raw, 1)
                    if norm:
                        if k == 0:
                            e.wait_ge(s_rec, s)
                        e.tensor_tensor(hf[o][:, k, :], hf[o][:, k, :], sr[:, :], ALU.mult).then_inc(h_norm, 1)
                        if k >= 1:
                            low(k - 1)
                if norm:
                    low(5)

            def first(e, j):
                hi = float(np.float16(H_SCALE / CH)); lo = H_SCALE / CH - hi
                for u in (0, 1):
                    e.memset(hf[u][:, :, :], H_SCALE / CH)
                    e.memset(hh[u][:, :, :], hi)
                    m = e.memset(hl[u][:, :, :], lo)
                m.then_inc(h_init, 1)
                e.wait_ge(h_init, j + 1)
                for u in (0, 1):
                    e.wait_ge(x_loaded[u], 96 * j + 96)

            def last(e, j):
                s = SLOTS * j + SLOTS
                e.wait_ge(total, s)
                e.tensor_scalar(sc[:, :], PS[:, :], EPS * X_SCALE / H_SCALE, None, ALU.max).then_inc(s_clamp, 1)
                e.wait_ge(s_inv, s)
                e.tensor_tensor(stt[:, :], sc[:, :], sy[:, :], ALU.mult).then_inc(s_newt, 1)
                e.wait_ge(s_newt, s)
                e.scalar_tensor_tensor(sr[:, :], stt[:, :], 2.0, sy[:, :], ALU.subtract, ALU.mult, reverse0=True).then_inc(s_rec, 1)
                e.wait_ge(s_rec, s)
                for k in range(6):
                    e.tensor_tensor(hf[1][:, k, :], hf[1][:, k, :], sr[:, :], ALU.mult).then_inc(h_norm, 1)
                for u in (0, 1):
                    e.wait_ge(h_stored[u], 96 * j + 96)
            schedule(dve, slot, last, first)

        @block.tensor
        def _(pe):
            pe.wait_ge(w_placed, 48)
            pe.wait_ge(id_done, 1)
            w1f = w1[:, :, :, :, :, :].rearrange("p h a b g m -> p (h a b g) m")
            for q in range(12):
                if q >= 4:
                    pe.wait_ge(w_copied, q - 3)
                for r in range(4):
                    mm = pe.transpose(PT(q)[:, 128 * r:128 * r + 128], w1f[:, 4 * q + r, :], ident[:, :])
                mm.then_inc(w_turned, 1)
            pe.wait_ge(w_copied, 12)
            pe.wait_ge(blk_done, 1)
            NEAR = [(a, b) for a in (0, 1) for b in (0, 1)]
            PASSES = ((0, 0), (1, 0), (0, 1))

            def reconstruct(u, k):
                out = [P1[k % 2][:, h, 0:B_COLS // 2].rearrange("p (i r c) -> p i r c", i=2, r=BR) for h in (0, 1)]
                for a, b in NEAR:
                    for wp, dp in PASSES:
                        for h in (0, 1):
                            src = (hh, hl)[dp][u][:, k, 256 * h:256 * h + 256]
                            mm = pe.matmul(out[h][:, :, 1 - a:1 - a + AR, 1 - b:1 - b + AC], w1[:, wp, a, b, k, :],
                                           src, start=(a, b, wp, dp) == (0, 0, 0, 0), stop=(a, b, wp, dp) == (1, 1, 0, 1), skip_group_check=True)
                mm.then_inc(recon, 1)

            def correlate(k):
                for a, b in NEAR:
                    for wp, dp in PASSES:
                        mm = pe.matmul(P2[k % 3][:, :], w2[:, wp, a, b, k, :],
                                       (nh, nl)[dp][:, k, :, 1 - a:1 - a + AR, 1 - b:1 - b + AC],
                                       start=(a, b, wp, dp) == (0, 0, 0, 0), stop=(a, b, wp, dp) == (1, 1, 0, 1))
                mm.then_inc(ratio, 1)

            def sum_up(e, u, s):
                e.wait_ge(summed, 5 * s)
                e.matmul(PS[:, :], blk[:, :, :].rearrange("p x c -> p (x c)"), acc[u][:, :], start=True, stop=True).then_inc(total, 1)

            def slot(e, j, u, s, norm, m=0, init=False):
                n = 6 * s
                for k in range(6):
                    if norm or k >= 2:
                        e.wait_ge(clamped, n + k - 1)
                    if norm is True and not init:
                        e.wait_ge(h_lo, 6 * m - 12 + k + 1)
                    reconstruct(u, k)
                    if norm and k == 2:
                        sum_up(e, 1 - u, s)
                for k in range(6):
                    e.wait_ge(nu_lo, n + k + 1)
                    if norm or k >= 3:
                        e.wait_ge(h_raw, n + k - 2)
                    correlate(k)

            with pe.Fori(0, PAIRS) as j:
                pe.wait_ge(h_init, j + 1)
                slot(pe, j, 0, SLOTS * j, False)
                slot(pe, j, 1, SLOTS * j + 1, True, 0, init=True)
                slot(pe, j, 0, SLOTS * j + 2, True, (SLOTS - 1) * j + 2)
                with pe.Fori(1, ITERS - 1) as i:
                    slot(pe, j, 1, SLOTS * j + 2 * i + 1, True, (SLOTS - 1) * j + 2 * i + 1)
                    slot(pe, j, 0, SLOTS * j + 2 * i + 2, True, (SLOTS - 1) * j + 2 * i + 2)
                slot(pe, j, 1, SLOTS * j + 2 * ITERS - 1, True, (2 * ITERS - 1) * j + 2 * ITERS - 1)
                sum_up(pe, 1, SLOTS * j + SLOTS)


HEADS, KD = 8, 32
MQ, HID = HEADS * KD, 4 * CH
PIX = HW * HW
HALF = PIX // 2
TAPS = 9


def attention_block(nc, x_in, wq, sq, bq, wkv, skv, bkv, wp, sp_, bp, w1, s1, b1, wdw, bdw, w2, s2, b2, g1, be1, x2_dram, xn_dram):
    ctx = ExitStack()
    with ctx:
        sb = lambda n, s, d=F32: ctx.enter_context(nc.sbuf_tensor("at_" + n, s, d))
        s_w_lo = ctx.enter_context(nc.semaphore("at_w_lo"))
        s_w_loaded = ctx.enter_context(nc.semaphore("at_w_loaded"))
        s_x_lo = ctx.enter_context(nc.semaphore("at_x_lo"))
        s_x_loaded = [ctx.enter_context(nc.semaphore(f"at_x_loaded{i}")) for i in range(2)]
        s_x1 = ctx.enter_context(nc.semaphore("at_x1"))
        s_x2 = ctx.enter_context(nc.semaphore("at_x2"))
        s_x2_stored = [ctx.enter_context(nc.semaphore(f"at_x2_stored{i}")) for i in range(2)]
        s_xb = ctx.enter_context(nc.semaphore("at_xb"))
        s_xn_stored = [ctx.enter_context(nc.semaphore(f"at_xn_stored{i}")) for i in range(2)]
        s_ones_row = ctx.enter_context(nc.semaphore("at_ones_row"))
        s_pz = ctx.enter_context(nc.semaphore("at_pz"))
        s_pc = ctx.enter_context(nc.semaphore("at_pc"))
        s_start = ctx.enter_context(nc.semaphore("at_start"))
        s_x_hi = ctx.enter_context(nc.semaphore("at_x_hi"))
        s_q = ctx.enter_context(nc.semaphore("at_q"))
        s_kv = ctx.enter_context(nc.semaphore("at_kv"))
        s_hd = ctx.enter_context(nc.semaphore("at_hd"))
        s_hd_hi = ctx.enter_context(nc.semaphore("at_hd_hi"))
        s_mlp = ctx.enter_context(nc.semaphore("at_mlp"))
        s_hd_lo = ctx.enter_context(nc.semaphore("at_hd_lo"))
        s_e_hi = ctx.enter_context(nc.semaphore("at_e_hi"))
        s_at = ctx.enter_context(nc.semaphore("at_at"))
        s_e_lo = ctx.enter_context(nc.semaphore("at_e_lo"))
        s_a_hi = ctx.enter_context(nc.semaphore("at_a_hi"))
        s_proj = ctx.enter_context(nc.semaphore("at_proj"))
        s_a_lo = ctx.enter_context(nc.semaphore("at_a_lo"))
        s_x1_hi = ctx.enter_context(nc.semaphore("at_x1_hi"))
        s_conv = ctx.enter_context(nc.semaphore("at_conv"))
        s_x1_lo = ctx.enter_context(nc.semaphore("at_x1_lo"))
        s_centred = ctx.enter_context(nc.semaphore("at_centred"))
        s_sqr = ctx.enter_context(nc.semaphore("at_sqr"))
        s_var = ctx.enter_context(nc.semaphore("at_var"))
        s_va = ctx.enter_context(nc.semaphore("at_va"))
        s_vl = ctx.enter_context(nc.semaphore("at_vl"))
        s_vy = ctx.enter_context(nc.semaphore("at_vy"))
        s_nd = ctx.enter_context(nc.semaphore("at_nd"))
        s_nl = ctx.enter_context(nc.semaphore("at_nl"))
        s_ny = ctx.enter_context(nc.semaphore("at_ny"))
        s_e32 = ctx.enter_context(nc.semaphore("at_e32"))
        s_ss = ctx.enter_context(nc.semaphore("at_ss"))
        s_s_y = ctx.enter_context(nc.semaphore("at_s_y"))
        s_s_l = ctx.enter_context(nc.semaphore("at_s_l"))
        s_s_r = ctx.enter_context(nc.semaphore("at_s_r"))
        s_a32 = ctx.enter_context(nc.semaphore("at_a32"))
        s_kcopy = ctx.enter_context(nc.semaphore("at_kcopy"))
        s_kt = ctx.enter_context(nc.semaphore("at_kt"))
        s_kt_psum = ctx.enter_context(nc.semaphore("at_kt_psum"))
        s_kexp = ctx.enter_context(nc.semaphore("at_kexp"))
        s_q_max = ctx.enter_context(nc.semaphore("at_q_max"))
        s_q_spread = ctx.enter_context(nc.semaphore("at_q_spread"))
        s_ones_in = ctx.enter_context(nc.semaphore("at_ones_in"))
        s_w_scaled = ctx.enter_context(nc.semaphore("at_w_scaled"))
        s_turned = ctx.enter_context(nc.semaphore("at_turned"))
        s_tap = ctx.enter_context(nc.semaphore("at_tap"))
        s_w_hi = ctx.enter_context(nc.semaphore("at_w_hi"))
        s_vb = ctx.enter_context(nc.semaphore("at_vb"))
        s_vr = ctx.enter_context(nc.semaphore("at_vr"))
        s_xnorm = ctx.enter_context(nc.semaphore("at_xnorm"))
        s_xaff = ctx.enter_context(nc.semaphore("at_xaff"))
        s_xm = ctx.enter_context(nc.semaphore("at_xm"))
        s_xsum = ctx.enter_context(nc.semaphore("at_xsum"))
        s_nt = ctx.enter_context(nc.semaphore("at_nt"))
        s_nr = ctx.enter_context(nc.semaphore("at_nr"))
        s_qt = ctx.enter_context(nc.semaphore("at_qt"))
        s_s_t = ctx.enter_context(nc.semaphore("at_s_t"))
        s_kmax = ctx.enter_context(nc.semaphore("at_kmax"))
        s_nkmax = ctx.enter_context(nc.semaphore("at_nkmax"))
        s_krec = ctx.enter_context(nc.semaphore("at_krec"))
        s_ctx = ctx.enter_context(nc.semaphore("at_ctx"))
        s_cs = ctx.enter_context(nc.semaphore("at_cs"))
        s_bd = ctx.enter_context(nc.semaphore("at_bd"))

        wq_r = sb("wq_r", [128, 2, CH + 1]); wkv_r = sb("wkv_r", [32, CH + 1]); w1_r = sb("w1_r", [128, 3, CH + 1])
        wp_r = sb("wp_r", [CH, MQ]); w2_r = sb("w2_r", [CH, HID])
        sq_c = sb("sq_c", [128, 2]); skv_c = sb("skv_c", [32, 1]); s1_c = sb("s1_c", [128, 3]); sp_c = sb("sp_c", [CH, 1]); s2_c = sb("s2_c", [CH, 1])
        bp_c = sb("bp_c", [CH, 1]); b2_c = sb("b2_c", [CH, 1]); bdw_c = sb("bdw_c", [128, 3]); wdw_c = sb("wdw_c", [128, 3, TAPS])
        g1_c = sb("g1_c", [CH, 1]); be1_c = sb("be1_c", [CH, 1])
        stage = [sb(f"stage{i}", [128, CH + 1]) for i in range(4)]
        wqT = [sb(f"wqT{h}", [CH + 1, MQ], F16) for h in (0, 1)]
        wkvT = [sb(f"wkvT{h}", [CH + 1, KD], F16) for h in (0, 1)]
        w1T = [sb(f"w1T{h}", [CH + 1, 3, TAPS, 128], F16) for h in (0, 1)]
        wpT = [sb(f"wpT{h}", [128, 2, CH], F16) for h in (0, 1)]
        w2T = [sb(f"w2T{h}", [128, 3, CH], F16) for h in (0, 1)]
        W_LOADED = []
        ident = sb("ident", [128, 128]); minus_i = sb("minus_i", [128, 128], BF16)
        ones_k = sb("ones_k", [128, 4, KD], F16)
        centre = sb("centre", [CH, CH]); mean_w = sb("mean_w", [CH, CH]); sum_w = sb("sum_w", [CH, CH])
        eps_c = sb("eps_c", [CH, 1])
        x32 = [sb(f"x32_{p}", [CH + 1, PIX]) for p in (0, 1)]
        x16 = [sb(f"x16_{h}", [CH + 1, PIX], F16) for h in (0, 1)]
        kk = sb("kk", [64, PIX]); kt = sb("kt", [128, 8, 64])
        kmax = sb("kmax", [32, 1]); nkmax = sb("nkmax", [32, 1]); ksum = sb("ksum", [32, 1]); krec = sb("krec", [32, 1])
        cs = sb("cs", [32, 32]); bd = [sb(f"bd{h}", [128, 128], F16) for h in (0, 1)]
        qm = sb("qm", [128, 8, HEADS], BF16)
        qe = sb("qe", [128, 8, HEADS, KD], BF16)
        e32 = [sb(f"e32_{i}", [128, HALF]) for i in (0, 1)]
        e16 = [sb(f"e16_{h}", [128, 4, HALF], F16) for h in (0, 1)]
        sl = sb("sl", [128, HALF]); sy = [sb(f"sy{i}", [128, HALF]) for i in (0, 1)]; st = sb("st", [128, HALF]); sr = sb("sr", [128, HALF])
        a32 = [sb(f"a32_{i}", [128, HALF]) for i in (0, 1)]
        a16 = [sb(f"a16_{h}", [128, 4, HALF], F16) for h in (0, 1)]
        x1 = [sb(f"x1_{p}", [CH, PIX]) for p in (0, 1)]
        xp = [[sb(f"xp{p}_{h}", [CH + 1, HW + 2, HW + 2], F16) for h in (0, 1)] for p in (0, 1)]
        hd32 = [sb(f"hd32_{i}", [128, HALF]) for i in (0, 1)]
        hd16 = [sb(f"hd16_{h}", [128, 6, HALF], F16) for h in (0, 1)]
        x2 = [sb(f"x2_{p}", [CH, HALF]) for p in (0, 1)]
        sqr = sb("sqr", [CH, HALF]); vl = sb("vl", [CH, HALF]); vy = sb("vy", [CH, HALF]); va = sb("va", [CH, HALF]); vb = sb("vb", [CH, HALF]); vr = sb("vr", [CH, HALF])
        xm = [sb(f"xm{i}", [CH, HALF]) for i in (0, 1)]
        nd = sb("nd", [CH, HALF]); nl = sb("nl", [CH, HALF]); ny = sb("ny", [CH, HALF]); nt = sb("nt", [CH, HALF]); nr = sb("nr", [CH, HALF])
        xb = [sb(f"xb{p}", [CH, PX, PY, BR, BC]) for p in (0, 1)]
        PC = [ctx.enter_context(nc.psum_tensor(f"at_PC{i}", [128, 512], F32)) for i in (0, 1)]
        PL = [ctx.enter_context(nc.psum_tensor(f"at_PL{i}", [128, 512], F32)) for i in (0, 1)]
        PA = ctx.enter_context(nc.psum_tensor("at_PA", [128, 2, 512], F32))
        PB = ctx.enter_context(nc.psum_tensor("at_PB", [128, 2, 512], F32))
        PBf = PB[:, :, :].rearrange("p a b -> p (a b)")
        turns = []
        for m in (0, 1):
            turns.append((wq_r[:, m, :], 128, CH + 1, wqT[0][:, 128 * m:128 * m + 128], wqT[1][:, 128 * m:128 * m + 128]))
        turns.append((wkv_r[:, :], 32, CH + 1, wkvT[0][:, :], wkvT[1][:, :]))
        for m in (0, 1):
            turns.append((wp_r[:, 128 * m:128 * m + 128], CH, 128, wpT[0][:, m, :], wpT[1][:, m, :]))
        for m in range(3):
            turns.append((w2_r[:, 128 * m:128 * m + 128], CH, 128, w2T[0][:, m, :], w2T[1][:, m, :]))
        plain = len(turns)
        for m in range(3):
            for t in range(TAPS):
                turns.append((stage[(9 * m + t) % 4][:, :], 128, CH + 1, w1T[0][:, m, t, :], w1T[1][:, m, t, :]))
        NT = len(turns)
        turn_bank = lambda q: (PA[:, 0, :], PA[:, 1, :], PB[:, 0, :], PB[:, 1, :])[q % 4]
        block = ctx.enter_context(nc.Block())


        def images(e, step, tail):
            step(e, -1, 1, -1, False, True, False)
            step(e, 0, 0, 0, True, True, False)
            step(e, 1, 1, 0, True, True, True)
            with e.Fori(1, NIMG // 2 - 1) as t:
                step(e, 2 * t, 0, t, True, True, True)
                step(e, 2 * t + 1, 1, t, True, True, True)
            t = NIMG // 2 - 1
            step(e, 2 * t, 0, t, True, True, True)
            step(e, 2 * t + 1, 1, t, True, False, True)
            tail(e)

        @block.sync
        def _(e):
            flat = lambda ap: ap.rearrange("(a n) -> a n", n=1)
            n = 0
            for dst, src in (
                [(wq_r[:, m, 0:CH], wq[128 * m:128 * m + 128, :]) for m in (0, 1)] + [(wq_r[:, m, CH:], flat(bq[128 * m:128 * m + 128])) for m in (0, 1)]
                + [(sq_c[:, m:m + 1], flat(sq[128 * m:128 * m + 128])) for m in (0, 1)]
                + [(wkv_r[:, 0:CH], wkv), (wkv_r[:, CH:], flat(bkv)), (skv_c[:, :], flat(skv))]
                + [(w1_r[:, m, 0:CH], w1[128 * m:128 * m + 128, :]) for m in range(3)] + [(w1_r[:, m, CH:], flat(b1[128 * m:128 * m + 128])) for m in range(3)]
                + [(s1_c[:, m:m + 1], flat(s1[128 * m:128 * m + 128])) for m in range(3)] + [(bdw_c[:, m:m + 1], flat(bdw[128 * m:128 * m + 128])) for m in range(3)]
                + [(wdw_c[:, m, :], wdw[128 * m:128 * m + 128].rearrange("o i a b -> o (i a b)")) for m in range(3)]
                + [(wp_r[:, :], wp), (w2_r[:, :], w2), (sp_c[:, :], flat(sp_)), (s2_c[:, :], flat(s2)), (bp_c[:, :], flat(bp)), (b2_c[:, :], flat(b2)),
                   (g1_c[:, :], flat(g1)), (be1_c[:, :], flat(be1))]
            ):
                e.dma_start(dst, src).then_inc(s_w_loaded, 16)
                n += 16
            W_LOADED.append(n)

            def step(e, i, p, t, conv, att, before):
                if conv and att:
                    e.wait_ge(s_x1, 2 * (i + 1))
                    if not isinstance(i, int) or i + 2 < NIMG:
                        e.dma_start(x32[p][0:CH, :], x_in[bass.ds(i + 2, 1)].rearrange("a c n -> (a c) n")).then_inc(s_x_loaded[p], 16)
                if before:
                    stores(e, i - 1, 1 - p)
            def stores(e, i, p):
                for h in (0, 1):
                    e.wait_ge(s_x2, 2 * i + h + 1)
                    e.dma_start(x2_dram[bass.ds(i, 1), :, HALF * h:HALF * h + HALF].rearrange("a c n -> (a c) n"), x2[h][:, :]).then_inc(s_x2_stored[h], 16)
                e.wait_ge(s_xb, 8 * (i + 1))
                for j in range(8):
                    e.dma_start(xn_dram[bass.ds(i, 1), :, GC * j:GC * j + GC, :].rearrange("a g c n -> (a g) c n"),
                                xb[p][:, j // 2, j % 2, :, :].rearrange("c r k -> c (r k)")).then_inc(s_xn_stored[p], 16)
            for p in (0, 1):
                e.wait_ge(s_ones_row, 1)
                e.dma_start(x32[p][0:CH, :], x_in[p]).then_inc(s_x_loaded[p], 16)
            images(e, step, lambda e: stores(e, NIMG - 1, 1))
            for p in (0, 1):
                e.wait_ge(s_x2_stored[p], 16 * NIMG)
                e.wait_ge(s_xn_stored[p], 16 * 8 * (NIMG // 2))

        @block.gpsimd
        def _(e):
            for t, v in ((ident, 1.0), (minus_i, -1.0)):
                e.memset(t[:, :], 0.0).then_inc(s_pz, 1)
            e.memset(centre[:, :], -1.0 / CH).then_inc(s_pz, 1)
            e.memset(ones_k[:, :, :], 1.0).then_inc(s_pz, 1)
            e.wait_ge(s_pz, 4)
            for t, v, r in ((ident, 1.0, 128), (minus_i, -1.0, 128), (centre, 1.0 - 1.0 / CH, CH)):
                e.affine_select(out=t[:, :], in_=t[:, :], compare_op=ALU.not_equal, fill=v, base=0, pattern=[[-1, r]], channel_multiplier=1).then_inc(s_pc, 1)
            e.affine_select(out=ones_k[:, :, :], in_=ones_k[:, :, :], compare_op=ALU.is_ge, fill=0.0, base=0, pattern=[[-KD, 4], [0, KD]], channel_multiplier=1).then_inc(s_pc, 1)
            e.wait_ge(s_pc, 4)
            e.affine_select(out=ones_k[:, :, :], in_=ones_k[:, :, :], compare_op=ALU.is_ge, fill=0.0, base=KD - 1, pattern=[[KD, 4], [0, KD]], channel_multiplier=-1).then_inc(s_pc, 1)
            e.wait_ge(s_start, 1)

            def step(e, i, p, t, conv, att, before):
                o = 1 - p; a = i + 1; ta = t + p
                first = isinstance(i, int) and i < 0

                def hidden_low(h, m):
                    u = 3 * h + m
                    e.wait_ge(s_hd_hi, 6 * i + u + 1)
                    if before or u >= 6:
                        e.wait_ge(s_mlp, 2 * i + h - 1)
                    e.tensor_tensor(hd16[1][:, u, :], hd32[u % 2][:, :], hd16[0][:, u, :], ALU.subtract).then_inc(s_hd_lo, 1)

                def e_low(v):
                    e.wait_ge(s_e_hi, 4 * a + v + 1)
                    if not first:
                        e.wait_ge(s_at, 4 * a + v - 3)
                    e.tensor_tensor(e16[1][:, v, :], e32[v % 2][:, :], e16[0][:, v, :], ALU.subtract).then_inc(s_e_lo, 1)

                def a_low(v):
                    e.wait_ge(s_a_hi, 4 * a + v + 1)
                    if not first:
                        e.wait_ge(s_proj, 2 * a)
                    e.tensor_tensor(a16[1][:, v, :], a32[v % 2][:, :], a16[0][:, v, :], ALU.subtract).then_inc(s_a_lo, 1)

                if att:
                    e.wait_ge(s_x_hi, a + 1)
                    if not first:
                        e.wait_ge(s_q, 4 * a)
                    e.tensor_tensor(x16[1][:, :], x32[o][:, :], x16[0][:, :], ALU.subtract).then_inc(s_x_lo, 1)
                if conv: hidden_low(0, 0)
                if conv: hidden_low(0, 1)
                if att: e_low(0); e_low(1)
                if conv: hidden_low(0, 2)
                if att: e_low(2); e_low(3)
                if conv: hidden_low(1, 0)
                if att: a_low(0); a_low(1)
                if conv: hidden_low(1, 1)
                if att: a_low(2); a_low(3)
                if conv: hidden_low(1, 2)
                if att:
                    for h in (0, 1):
                        e.wait_ge(s_x1_hi, 2 * a + h + 1)
                        if not first and not (isinstance(i, int) and i < 1):
                            e.wait_ge(s_conv, 6 * (a - 1))
                        inner = lambda t_: t_[0:CH, 1 + 16 * h:17 + 16 * h, 1:HW + 1]
                        e.tensor_tensor(inner(xp[o][1]), x1[o][:, HALF * h:HALF * h + HALF].rearrange("p (r c) -> p r c", c=HW),
                                        inner(xp[o][0]), ALU.subtract).then_inc(s_x1_lo, 1)
            images(e, step, lambda e: None)

        @block.scalar
        def _(e):
            e.preload_act_table_set("natural_log_exp_and_others")
            e.wait_ge(s_start, 1)

            def step(e, i, p, t, conv, att, before):
                o = 1 - p; a = i + 1; ta = t + p
                first = isinstance(i, int) and i < 0

                def relu(h, m):
                    u = 3 * h + m
                    e.wait_ge(s_conv, 6 * i + u + 1)
                    if before or u >= 2:
                        e.wait_ge(s_hd_lo, 6 * i + u - 1)
                    e.activation(hd32[u % 2][:, :], PC[u % 2][:, :], ACT.Relu, bias=bdw_c[:, m:m + 1]).then_inc(s_hd, 1)

                def norm(H, n):
                    if n == 0:
                        e.wait_ge(s_centred, H + 1)
                        e.activation(sqr[:, :], PL[1][0:CH, :], ACT.Square).then_inc(s_sqr, 1)
                    if n == 1:
                        e.wait_ge(s_var, H + 1)
                        e.activation(vl[:, :], PL[0][0:CH, :], ACT.Ln, bias=eps_c[:, :]).then_inc(s_vl, 1)
                        e.wait_ge(s_vl, H + 1)
                        e.activation(vy[:, :], vl[:, :], ACT.Exp, scale=-0.5).then_inc(s_vy, 1)
                    if n == 2:
                        e.wait_ge(s_nd, H + 1)
                        e.activation(nl[:, :], nd[:, :], ACT.Ln).then_inc(s_nl, 1)
                        e.wait_ge(s_nl, H + 1)
                        e.activation(ny[:, :], nl[:, :], ACT.Exp, scale=-1.0).then_inc(s_ny, 1)

                def q_exp(v):
                    e.wait_ge(s_q, 4 * a + v + 1)
                    if not first or v >= 2:
                        e.wait_ge(s_e_lo, 4 * a + v - 1)
                    e.activation(e32[v % 2][:, :], PB[:, v % 2, :], ACT.Exp).then_inc(s_e32, 1)
                    e.wait_ge(s_e32, 4 * a + v + 1)
                    if not first:
                        e.wait_ge(s_at, 4 * a + v - 3)
                    e.activation(e16[0][:, v, :], e32[v % 2][:, :], ACT.Copy).then_inc(s_e_hi, 1)

                def s_inv(v):
                    e.wait_ge(s_ss, 4 * a + v + 1)
                    if not first or v >= 1:
                        e.wait_ge(s_s_y, 4 * a + v)
                    e.activation(sl[:, :], PA[:, 0, :], ACT.Ln).then_inc(s_s_l, 1)
                    e.wait_ge(s_s_l, 4 * a + v + 1)
                    if not first or v >= 2:
                        e.wait_ge(s_s_r, 4 * a + v - 1)
                    e.activation(sy[v % 2][:, :], sl[:, :], ACT.Exp, scale=-1.0).then_inc(s_s_y, 1)

                def a_hi(v):
                    e.wait_ge(s_a32, 4 * a + v + 1)
                    if not first:
                        e.wait_ge(s_proj, 2 * a)
                    e.activation(a16[0][:, v, :], a32[v % 2][:, :], ACT.Copy).then_inc(s_a_hi, 1)

                H = 2 * i if conv else None
                if att:
                    e.wait_ge(s_x_loaded[o], 16 * (ta + 1))
                    if not first:
                        e.wait_ge(s_q, 4 * a); e.wait_ge(s_x_lo, a)
                    e.activation(x16[0][:, :], x32[o][:, :], ACT.Copy).then_inc(s_x_hi, 1)
                if conv: relu(0, 0)
                if att:
                    e.wait_ge(s_kcopy, a + 1)
                    if not first:
                        e.wait_ge(s_kt_psum, a)
                    e.activation(kk[0:32, :], PA[0:32, :, :].rearrange("p a b -> p (a b)"), ACT.Exp, bias=nkmax[:, :], accum_out=ksum[:, :]).then_inc(s_kexp, 1)
                    for r in (0, 1):
                        e.wait_ge(s_q_max, 2 * a + r + 1)
                        e.activation(qe[:, 4 * r:4 * r + 4, :, :].rearrange("p t h k -> p (t h) k"),
                                     qm[:, 4 * r:4 * r + 4, :].rearrange("p t h -> p (t h)").unsqueeze(2).to_broadcast([128, 32, KD]), ACT.Copy).then_inc(s_q_spread, 1)
                if before: norm(H - 2, 2)
                if conv: relu(0, 1)
                if before: norm(H - 1, 0)
                if att: q_exp(0); q_exp(1)
                if conv: relu(0, 2)
                if before: norm(H - 1, 1)
                if att: q_exp(2); q_exp(3)
                if conv: relu(1, 0)
                if before: norm(H - 1, 2)
                if att: s_inv(0); s_inv(1); a_hi(0)
                if conv: relu(1, 1); norm(H, 0)
                if att: a_hi(1); s_inv(2); s_inv(3); a_hi(2)
                if conv: relu(1, 2); norm(H, 1)
                if att:
                    a_hi(3)
                    for h in (0, 1):
                        e.wait_ge(s_x1, 2 * a + h + 1)
                        if not first and not (isinstance(i, int) and i < 1):
                            e.wait_ge(s_conv, 6 * (a - 1))
                        e.activation(xp[o][0][0:CH, 1 + 16 * h:17 + 16 * h, 1:HW + 1],
                                     x1[o][:, HALF * h:HALF * h + HALF].rearrange("p (r c) -> p r c", c=HW), ACT.Copy).then_inc(s_x1_hi, 1)

            def tail(e):
                H = 2 * NIMG - 2
                def norm(H, n):
                    if n == 0:
                        e.wait_ge(s_centred, H + 1)
                        e.activation(sqr[:, :], PL[1][0:CH, :], ACT.Square).then_inc(s_sqr, 1)
                    if n == 1:
                        e.wait_ge(s_var, H + 1)
                        e.activation(vl[:, :], PL[0][0:CH, :], ACT.Ln, bias=eps_c[:, :]).then_inc(s_vl, 1)
                        e.wait_ge(s_vl, H + 1)
                        e.activation(vy[:, :], vl[:, :], ACT.Exp, scale=-0.5).then_inc(s_vy, 1)
                    if n == 2:
                        e.wait_ge(s_nd, H + 1)
                        e.activation(nl[:, :], nd[:, :], ACT.Ln).then_inc(s_nl, 1)
                        e.wait_ge(s_nl, H + 1)
                        e.activation(ny[:, :], nl[:, :], ACT.Exp, scale=-1.0).then_inc(s_ny, 1)
                norm(H, 2); norm(H + 1, 0); norm(H + 1, 1); norm(H + 1, 2)
            images(e, step, tail)

        @block.vector
        def _(e):
            for p in (0, 1):
                e.memset(x32[p][CH:CH + 1, :], 1.0)
                e.memset(xb[p][:, :, :, :, :], 0.0)
                for h in (0, 1):
                    last = e.memset(xp[p][h][:, :, :], 0.0)
            for h in (0, 1):
                last = e.memset(bd[h][:, :], 0.0)
            e.memset(mean_w[:, :], 1.0 / CH); e.memset(sum_w[:, :], 1.0 / X_SCALE)
            e.memset(eps_c[:, :], 1e-6).then_inc(s_ones_row, 1)
            e.wait_ge(s_ones_row, 1)
            for p in (0, 1):
                e.memset(xp[p][0][CH:CH + 1, 1:HW + 1, 1:HW + 1], 1.0).then_inc(s_ones_in, 1)
            e.wait_ge(s_w_loaded, W_LOADED[0])
            for t_, c in [(wq_r[:, m, 0:CH], sq_c[:, m:m + 1]) for m in (0, 1)] + [(wkv_r[:, 0:CH], skv_c[:, :])] + \
                    [(w1_r[:, m, 0:CH], s1_c[:, m:m + 1]) for m in range(3)] + [(wp_r[:, :], sp_c[:, :]), (w2_r[:, :], s2_c[:, :])]:
                e.tensor_scalar(t_, t_, c, None, ALU.mult).then_inc(s_w_scaled, 1)
            e.wait_ge(s_w_scaled, 8)
            for q, (src, rows, k, hi, lo) in enumerate(turns):
                def tap(z):
                    m, t = divmod(z, TAPS)
                    if z >= 4:
                        e.wait_ge(s_turned, plain + z - 3)
                    e.tensor_scalar(stage[z % 4][:, :], w1_r[:, m, :], wdw_c[:, m, t:t + 1], None, ALU.mult).then_inc(s_tap, 1)
                if q == 0:
                    for z in range(3): tap(z)
                if q >= plain and q - plain + 3 < 27:
                    tap(q - plain + 3)
                e.wait_ge(s_turned, q + 1)
                e.tensor_copy(hi, turn_bank(q)[0:k, 0:rows]).then_inc(s_w_hi, 1)
                e.wait_ge(s_w_hi, q + 1)
                e.tensor_tensor(lo, turn_bank(q)[0:k, 0:rows], hi, ALU.subtract).then_inc(s_w_lo, 1)
            e.wait_ge(s_w_lo, NT); e.wait_ge(s_ones_in, 2); e.wait_ge(s_pc, 5)
            e.memset(kmax[:, :], 0.0).then_inc(s_start, 1)
            e.wait_ge(s_start, 1)

            def x2_make(H, o_or_p, h):
                e.wait_ge(s_mlp, H + 1)
                e.scalar_tensor_tensor(x2[h][:, :], PL[0][0:CH, :], b2_c[:, :], x1[o_or_p][:, HALF * h:HALF * h + HALF], ALU.add, ALU.add).then_inc(s_x2, 1)

            def norm_scale(H):
                e.wait_ge(s_vy, H + 1)
                e.scalar_tensor_tensor(va[:, :], PL[0][0:CH, :], 1e-6, vy[:, :], ALU.add, ALU.mult).then_inc(s_va, 1)
                e.wait_ge(s_va, H + 1)
                e.tensor_tensor(vb[:, :], va[:, :], vy[:, :], ALU.mult).then_inc(s_vb, 1)
                e.wait_ge(s_vb, H + 1)
                e.scalar_tensor_tensor(vr[:, :], vb[:, :], 3.0, vy[:, :], ALU.subtract, ALU.mult).then_inc(s_vr, 1)
                e.wait_ge(s_vr, H + 1)
                e.scalar_tensor_tensor(va[:, :], PL[1][0:CH, :], -0.5, vr[:, :], ALU.mult, ALU.mult).then_inc(s_xnorm, 1)
                e.wait_ge(s_xnorm, H + 1)
                e.tensor_scalar(vb[:, :], va[:, :], g1_c[:, :], be1_c[:, :], ALU.mult, ALU.add).then_inc(s_xaff, 1)
                e.wait_ge(s_xaff, H + 1)

            def norm_floor(H, h):
                e.tensor_scalar(xm[h][:, :], vb[:, :], EPS, None, ALU.max).then_inc(s_xm, 1)

            def sum_clamp(H):
                e.wait_ge(s_xsum, H + 1)
                e.tensor_scalar(nd[:, :], PL[1][0:CH, :], EPS / X_SCALE, None, ALU.max).then_inc(s_nd, 1)

            def divide(H, h, p):
                e.wait_ge(s_ny, H + 1)
                e.tensor_tensor(nt[:, :], nd[:, :], ny[:, :], ALU.mult).then_inc(s_nt, 1)
                e.wait_ge(s_nt, H + 1)
                e.scalar_tensor_tensor(nr[:, :], nt[:, :], 2.0, ny[:, :], ALU.subtract, ALU.mult, reverse0=True).then_inc(s_nr, 1)
                e.wait_ge(s_nr, H + 1)
                for y in (0, 1):
                    r0 = 8 * h + (1 - y if y == 0 else 0)
                    v = lambda t_: t_[:, :].rearrange("c (r y n) -> c y r n", y=2, n=HW)[:, 1 - y]
                    for lo, xs_ in ((True, slice(0, 3)), (False, slice(3, 4))):
                        if lo:
                            w = lambda t_: v(t_).rearrange("c r (k x) -> c x r k", x=4)[:, 1:4]
                            out = xb[p][:, 0:3, y, r0:r0 + 8, 1:9]
                        else:
                            w = lambda t_: v(t_).rearrange("c r (k x) -> c x r k", x=4)[:, 0:1]
                            out = xb[p][:, 3:4, y, r0:r0 + 8, 0:8]
                        e.tensor_tensor(out, w(xm[h]), w(nr), ALU.mult).then_inc(s_xb, 1)

            def step(e, i, p, t, conv, att, before):
                o = 1 - p; a = i + 1; ta = t + p
                first = isinstance(i, int) and i < 0

                def hidden_hi(h, m):
                    u = 3 * h + m
                    e.wait_ge(s_hd, 6 * i + u + 1)
                    if before:
                        e.wait_ge(s_mlp, 2 * i + h - 1)
                    e.tensor_copy(hd16[0][:, u, :], hd32[u % 2][:, :]).then_inc(s_hd_hi, 1)

                def q_max(r):
                    e.wait_ge(s_qt, 2 * a + r + 1)
                    if not first:
                        e.wait_ge(s_q_spread, 2 * a)
                    e.tensor_reduce(qm[:, 4 * r:4 * r + 4, :].rearrange("p t h -> p (t h)"), PBf.rearrange("p (g k) -> p g k", k=KD), AX.X, ALU.max).then_inc(s_q_max, 1)

                def s_newton(v):
                    e.wait_ge(s_s_y, 4 * a + v + 1)
                    e.tensor_tensor(st[:, :], PA[:, 0, :], sy[v % 2][:, :], ALU.mult).then_inc(s_s_t, 1)
                    e.wait_ge(s_s_t, 4 * a + v + 1)
                    e.scalar_tensor_tensor(sr[:, :], st[:, :], 2.0, sy[v % 2][:, :], ALU.subtract, ALU.mult, reverse0=True).then_inc(s_s_r, 1)
                    e.wait_ge(s_s_r, 4 * a + v + 1); e.wait_ge(s_at, 4 * a + v + 1)
                    if not first or v >= 2:
                        e.wait_ge(s_a_lo, 4 * a + v - 1)
                    e.scalar_tensor_tensor(a32[v % 2][:, :], PA[:, 1, :], 0.0, sr[:, :], ALU.max, ALU.mult).then_inc(s_a32, 1)

                H = 2 * i if conv else None
                if att:
                    kv = PA[0:32, :, :].rearrange("p a b -> p (a b)")
                    e.wait_ge(s_kv, a + 1)
                    if not first:
                        e.wait_ge(s_kt_psum, a)
                    e.tensor_reduce(kmax[:, :], kv, AX.X, ALU.max).then_inc(s_kmax, 1)
                    e.wait_ge(s_kmax, a + 1)
                    e.tensor_scalar(nkmax[:, :], kmax[:, :], -1.0, None, ALU.mult).then_inc(s_nkmax, 1)
                    e.tensor_copy(kk[32:64, :], kv).then_inc(s_kcopy, 1)
                if conv: hidden_hi(0, 0)
                if before:
                    e.wait_ge(s_x2_stored[1], 16 * (i - 1)) if not (isinstance(i, int) and i < 2) else None
                    x2_make(H - 1, o, 1)
                    sum_clamp(H - 2)
                if att: q_max(0); q_max(1)
                if before:
                    if not (isinstance(i, int) and i < 3):
                        e.wait_ge(s_xn_stored[o], 128 * (t - 1 + p))
                    divide(H - 2, 0, o)
                if conv: hidden_hi(0, 1)
                if att:
                    e.wait_ge(s_kexp, a + 1)
                    e.reciprocal(krec[:, :], ksum[:, :]).then_inc(s_krec, 1)
                    e.wait_ge(s_kt_psum, a + 1)
                    if not first: e.wait_ge(s_ctx, a)
                    e.tensor_copy(kt[:, :, :].rearrange("p t n -> p (t n)"), PA[:, 0, :]).then_inc(s_kt, 1)
                if conv: hidden_hi(0, 2)
                if before:
                    norm_scale(H - 1)
                    norm_floor(H - 1, 1)
                if att:
                    e.wait_ge(s_ctx, a + 1); e.wait_ge(s_krec, a + 1)
                    e.tensor_scalar(cs[:, :], PA[0:32, 1, 0:32], krec[:, :], None, ALU.mult).then_inc(s_cs, 1)
                    e.wait_ge(s_cs, a + 1)
                    if not first: e.wait_ge(s_at, 4 * a)
                    for q in range(4):
                        s_ = slice(32 * q, 32 * q + 32)
                        e.tensor_copy(bd[0][s_, s_], cs[:, :]).then_inc(s_bd, 1)
                    e.wait_ge(s_bd, 8 * a + 1)
                    for q in range(4):
                        s_ = slice(32 * q, 32 * q + 32)
                        e.tensor_tensor(bd[1][s_, s_], cs[:, :], bd[0][0:32, 0:32], ALU.subtract).then_inc(s_bd, 1)
                if conv:
                    hidden_hi(1, 0)
                    if before: e.wait_ge(s_x2_stored[0], 16 * i)
                    x2_make(H, p, 0)
                if before: sum_clamp(H - 1); divide(H - 1, 1, o)
                if att: s_newton(0); s_newton(1)
                if conv: hidden_hi(1, 1)
                if att: s_newton(2); s_newton(3)
                if conv:
                    hidden_hi(1, 2)
                    norm_scale(H); norm_floor(H, 0)
                if att:
                    for h in (0, 1):
                        e.wait_ge(s_proj, 2 * a + h + 1)
                        e.scalar_tensor_tensor(x1[o][:, HALF * h:HALF * h + HALF], PB[0:CH, h, :], bp_c[:, :],
                                               x32[o][0:CH, HALF * h:HALF * h + HALF], ALU.add, ALU.add).then_inc(s_x1, 1)

            def tail(e):
                H = 2 * NIMG - 2
                e.wait_ge(s_x2_stored[1], 16 * (NIMG - 1))
                x2_make(H + 1, 1, 1)
                sum_clamp(H)
                e.wait_ge(s_xn_stored[1], 128 * (NIMG // 2 - 1))
                divide(H, 0, 1)
                norm_scale(H + 1); norm_floor(H + 1, 1)
                sum_clamp(H + 1); divide(H + 1, 1, 1)
            images(e, step, tail)

        @block.tensor
        def _(e):
            e.wait_ge(s_w_scaled, 8); e.wait_ge(s_pc, 5)
            for q, (src, rows, k, hi, lo) in enumerate(turns):
                if q >= 4: e.wait_ge(s_w_lo, q - 3)
                if q >= plain: e.wait_ge(s_tap, q - plain + 1)
                e.transpose(turn_bank(q)[0:k, 0:rows], src, ident[0:rows, 0:rows]).then_inc(s_turned, 1)
            e.wait_ge(s_start, 1)
            PASSES = ((0, 0), (1, 0), (0, 1))

            def mlp_out(H, h):
                e.wait_ge(s_hd_lo, 3 * H + 3)
                e.wait_ge(s_va, H)
                for m in range(3):
                    for wp_, dp in PASSES:
                        mm = e.matmul(PL[0][0:CH, :], w2T[wp_][:, m, :], hd16[dp][:, 3 * h + m, :], start=(m, wp_, dp) == (0, 0, 0), stop=(m, wp_, dp) == (2, 0, 1))
                mm.then_inc(s_mlp, 1)

            def centring(H, h):
                e.wait_ge(s_x2, H + 1)
                e.wait_ge(s_nd, H)
                e.matmul(PL[1][0:CH, :], centre[:, :], x2[h][:, :], start=True, stop=True).then_inc(s_centred, 1)

            def variance(H):
                e.wait_ge(s_sqr, H + 1)
                e.matmul(PL[0][0:CH, :], mean_w[:, :], sqr[:, :], start=True, stop=True).then_inc(s_var, 1)

            def x_sum(H, h):
                e.wait_ge(s_xm, H + 1)
                e.matmul(PL[1][0:CH, :], sum_w[:, :], xm[h][:, :], start=True, stop=True).then_inc(s_xsum, 1)

            def step(e, i, p, t, conv, att, before):
                o = 1 - p; a = i + 1
                first = isinstance(i, int) and i < 0

                def convolve(h, m):
                    u = 3 * h + m
                    if u in (0,):
                        e.wait_ge(s_x1_lo, 2 * i + 2)
                    if before or u >= 2:
                        e.wait_ge(s_hd, 6 * i + u - 1)
                    for tap in range(TAPS):
                        dy, dx = divmod(tap, 3)
                        for wp_, dp in PASSES:
                            mm = e.matmul(PC[u % 2][:, :], w1T[wp_][:, m, tap, :], xp[p][dp][:, 16 * h + dy:16 * h + dy + 16, dx:dx + HW],
                                          start=(tap, wp_, dp) == (0, 0, 0), stop=(tap, wp_, dp) == (TAPS - 1, 0, 1))
                    mm.then_inc(s_conv, 1)

                def q_rows(r):
                    if r == 0:
                        e.wait_ge(s_x_hi, a + 1)
                        if not first: e.wait_ge(s_x1, 2 * a)
                    else:
                        e.wait_ge(s_q_max, 2 * a + 1)
                    for n in range(4):
                        mm = e.matmul(PBf[:, 256 * n:256 * n + 256], x16[0][:, 128 * (4 * r + n):128 * (4 * r + n) + 128], wqT[0][:, :], start=n % 2 == 0, stop=n % 2 == 1, skip_group_check=True)
                    mm.then_inc(s_qt, 1)

                def q_cols(v):
                    h, m = divmod(v, 2)
                    e.wait_ge(s_q_spread, 2 * a + 2)
                    if v >= 2: e.wait_ge(s_e32, 4 * a + v - 1)
                    for wp_, dp in PASSES:
                        e.matmul(PB[:, v % 2, :], wqT[wp_][:, 128 * m:128 * m + 128], x16[dp][:, HALF * h:HALF * h + HALF], start=(wp_, dp) == (0, 0), stop=False)
                    for n in range(4):
                        mm = e.matmul(PB[:, v % 2, 128 * n:128 * n + 128], qe[:, 4 * h + n, 4 * m:4 * m + 4, :].rearrange("p a b -> p (a b)"),
                                      minus_i[:, :], start=False, stop=n == 3)
                    mm.then_inc(s_q, 1)

                def mix(v):
                    e.wait_ge(s_e_lo, 4 * a + v + 1)
                    if v == 0: e.wait_ge(s_bd, 8 * a + 8)
                    if v > 0: e.wait_ge(s_s_t, 4 * a + v)
                    for dp in (0, 1):
                        mm = e.matmul(PA[:, 0, :], ones_k[:, :, :].rearrange("p a b -> p (a b)"), e16[dp][:, v, :], start=dp == 0, stop=dp == 1)
                    mm.then_inc(s_ss, 1)
                    if v > 0: e.wait_ge(s_a32, 4 * a + v)
                    for wp_, dp in PASSES:
                        mm = e.matmul(PA[:, 1, :], bd[wp_][:, :], e16[dp][:, v, :], start=(wp_, dp) == (0, 0), stop=(wp_, dp) == (0, 1))
                    mm.then_inc(s_at, 1)

                if conv: convolve(0, 0)
                if before: mlp_out(2 * i - 1, 1); x_sum(2 * i - 2, 0)
                if att:
                    e.wait_ge(s_x_lo, a + 1)
                    if not first: e.wait_ge(s_a32, 4 * a)
                    for h in (0, 1):
                        for wp_, dp in PASSES:
                            mm = e.matmul(PA[0:KD, h, :], wkvT[wp_][:, :], x16[dp][:, HALF * h:HALF * h + HALF], start=(wp_, dp) == (0, 0), stop=(wp_, dp) == (0, 1))
                    mm.then_inc(s_kv, 1)
                    q_rows(0); q_rows(1)
                if conv: convolve(0, 1)
                if before: centring(2 * i - 1, 1)
                if att:
                    e.wait_ge(s_kexp, a + 1); e.wait_ge(s_kcopy, a + 1)
                    q_cols(0)
                    for n in range(8):
                        mm = e.transpose(PA[:, 0, 64 * n:64 * n + 64], kk[:, 128 * n:128 * n + 128], ident[0:64, 0:64])
                    mm.then_inc(s_kt_psum, 1)
                    q_cols(1)
                if conv: convolve(0, 2)
                if before: variance(2 * i - 1)
                if att:
                    e.wait_ge(s_kt, a + 1)
                    for n in range(8):
                        mm = e.matmul(PA[0:KD, 1, 0:KD], kt[:, n, 0:KD], kt[:, n, KD:2 * KD], start=n == 0, stop=n == 7)
                    mm.then_inc(s_ctx, 1)
                    q_cols(2); q_cols(3)
                if conv: convolve(1, 0); mlp_out(2 * i, 0)
                if before: x_sum(2 * i - 1, 1)
                if att: e.wait_ge(s_cs, a + 1); mix(0); mix(1)
                if conv: convolve(1, 1); centring(2 * i, 0)
                if att: mix(2); mix(3)
                if conv: convolve(1, 2); variance(2 * i)
                if att:
                    e.wait_ge(s_a_lo, 4 * a + 4)
                    for h in (0, 1):
                        for m in (0, 1):
                            for wp_, dp in PASSES:
                                mm = e.matmul(PB[0:CH, h, :], wpT[wp_][:, m, :], a16[dp][:, 2 * h + m, :], start=(m, wp_, dp) == (0, 0, 0), stop=(m, wp_, dp) == (1, 0, 1))
                        mm.then_inc(s_proj, 1)

            def tail(e):
                H = 2 * NIMG - 2
                mlp_out(H + 1, 1); x_sum(H, 0)
                centring(H + 1, 1); variance(H + 1); x_sum(H + 1, 1)
            images(e, step, tail)


UNITS = 4


def token_mlp(nc, x2_dram, h_dram, g2, be2, wf1, bf1, wf2, bf2, out):
    ctx = ExitStack()
    with ctx:
        sb = lambda n, s, d=F32: ctx.enter_context(nc.sbuf_tensor("ml_" + n, s, d))
        s_w_loaded = ctx.enter_context(nc.semaphore("ml_w_loaded"))
        s_y = ctx.enter_context(nc.semaphore("ml_y"))
        s_x_loaded = [ctx.enter_context(nc.semaphore(f"ml_x_loaded{i}")) for i in range(4)]
        s_h_loaded = [ctx.enter_context(nc.semaphore(f"ml_h_loaded{i}")) for i in range(4)]
        s_out = ctx.enter_context(nc.semaphore("ml_out"))
        s_stored = [ctx.enter_context(nc.semaphore(f"ml_stored{i}")) for i in range(2)]
        s_pz = ctx.enter_context(nc.semaphore("ml_pz"))
        s_pc = ctx.enter_context(nc.semaphore("ml_pc"))
        s_yn_hi = ctx.enter_context(nc.semaphore("ml_yn_hi"))
        s_yn = ctx.enter_context(nc.semaphore("ml_yn"))
        s_fc1 = ctx.enter_context(nc.semaphore("ml_fc1"))
        s_yn_lo = ctx.enter_context(nc.semaphore("ml_yn_lo"))
        s_g = ctx.enter_context(nc.semaphore("ml_g"))
        s_g_hi = ctx.enter_context(nc.semaphore("ml_g_hi"))
        s_fc2 = ctx.enter_context(nc.semaphore("ml_fc2"))
        s_g_lo = ctx.enter_context(nc.semaphore("ml_g_lo"))
        s_ready = ctx.enter_context(nc.semaphore("ml_ready"))
        s_hn = ctx.enter_context(nc.semaphore("ml_hn"))
        s_centred = ctx.enter_context(nc.semaphore("ml_centred"))
        s_var = ctx.enter_context(nc.semaphore("ml_var"))
        s_va = ctx.enter_context(nc.semaphore("ml_va"))
        s_sqr = ctx.enter_context(nc.semaphore("ml_sqr"))
        s_vy = ctx.enter_context(nc.semaphore("ml_vy"))
        s_vl = ctx.enter_context(nc.semaphore("ml_vl"))
        s_vr = ctx.enter_context(nc.semaphore("ml_vr"))
        s_mw = ctx.enter_context(nc.semaphore("ml_mw"))
        s_wg = ctx.enter_context(nc.semaphore("ml_wg"))
        s_wh = ctx.enter_context(nc.semaphore("ml_wh"))
        s_wl = ctx.enter_context(nc.semaphore("ml_wl"))
        s_bias = ctx.enter_context(nc.semaphore("ml_bias"))
        s_b1 = ctx.enter_context(nc.semaphore("ml_b1"))
        s_vb = ctx.enter_context(nc.semaphore("ml_vb"))

        w1r = sb("w1r", [CH, HID]); w1g = sb("w1g", [CH, HID]); w2r = sb("w2r", [128, 3, CH])
        w1 = [sb(f"w1_{h}", [CH, HID], F16) for h in (0, 1)]
        w2 = [sb(f"w2_{h}", [128, 3, CH], F16) for h in (0, 1)]
        g2c = sb("g2c", [CH, 1]); be2c = sb("be2c", [CH, 1]); bf1c = sb("bf1c", [128, 3]); bf2c = sb("bf2c", [CH, 1]); b1 = sb("b1", [128, 3])
        centre = sb("centre", [CH, CH]); mean_w = sb("mean_w", [CH, CH]); eps_c = sb("eps_c", [CH, 1])
        xt = [sb(f"xt{i}", [CH, PIX]) for i in range(4)]
        ht = [sb(f"ht{i}", [CH, PX, PY, AR, AC]) for i in range(4)]
        hn = [sb(f"hn{i}", [CH, PIX]) for i in range(2)]
        yt = [sb(f"yt{i}", [CH, PIX]) for i in range(4)]
        sqr = [sb(f"sqr{i}", [CH, HALF]) for i in range(2)]
        vl = sb("vl", [CH, HALF]); vy = [sb(f"vy{i}", [CH, HALF]) for i in range(2)]
        va = sb("va", [CH, HALF]); vb = sb("vb", [CH, HALF]); vr = sb("vr", [CH, HALF])
        yn = [sb(f"yn{i}", [CH, HALF]) for i in range(2)]
        y16 = [sb(f"y16_{h}", [CH, 2, UNITS, HALF], F16) for h in (0, 1)]
        g32 = [sb(f"g32_{i}", [128, HALF]) for i in range(3)]
        g16 = [sb(f"g16_{h}", [128, 6, HALF], F16) for h in (0, 1)]
        ot = [sb(f"ot{i}", [CH, HALF]) for i in range(2)]
        PX_ = [ctx.enter_context(nc.psum_tensor(f"ml_PX{i}", [128, 512], F32)) for i in (0, 1)]
        PV = [ctx.enter_context(nc.psum_tensor(f"ml_PV{i}", [128, 512], F32)) for i in (0, 1)]
        PG = [ctx.enter_context(nc.psum_tensor(f"ml_PG{i}", [128, 512], F32)) for i in range(3)]
        PO = ctx.enter_context(nc.psum_tensor("ml_PO", [128, 512], F32))
        block = ctx.enter_context(nc.Block())
        B = NIMG // 2
        flat = lambda ap: ap.rearrange("(a n) -> a n", n=1)

        def program(e, norm, mlp):
            norm(0, 0, True); norm(1, 1, True); mlp(0, 0, True)
            norm(2, 0, False); mlp(1, 1, False)
            with e.Fori(1, B // 2 - 1) as t:
                norm(2 * t + 1, 1, False); mlp(2 * t, 0, False)
                norm(2 * t + 2, 0, False); mlp(2 * t + 1, 1, False)
            norm(B - 1, 1, False); mlp(B - 2, 0, False); mlp(B - 1, 1, False)

        @block.sync
        def _(e):
            for dst, src in ((w1r[:, :], wf1), (w2r[:, :, :], wf2.rearrange("(m p) n -> p m n", p=128)), (g2c[:, :], flat(g2)), (be2c[:, :], flat(be2)),
                             (bf2c[:, :], flat(bf2)),
                             *((bf1c[:, m:m + 1], flat(bf1[128 * m:128 * m + 128])) for m in range(3))):
                e.dma_start(dst, src).then_inc(s_w_loaded, 16)

            def norm(b, p, early):
                for v in (0, 1):
                    i = 2 * p + v
                    if not early:
                        e.wait_ge(s_y, 2 * (b - 2) + v + 1)
                    e.dma_start(xt[i][:, :], x2_dram[bass.ds(2 * b + v, 1)].rearrange("a c n -> (a c) n")).then_inc(s_x_loaded[i], 16)
                    for j in range(8):
                        e.dma_start(ht[i][:, j // 2, j % 2, :, :].rearrange("c r k -> c (r k)"),
                                    h_dram[bass.ds(2 * b + v, 1), :, GC * j:GC * j + GC, :].rearrange("a g c n -> (a g) c n")).then_inc(s_h_loaded[i], 16)

            def mlp(b, p, early):
                for u in range(UNITS):
                    e.wait_ge(s_out, UNITS * b + u + 1)
                    e.dma_start(out[bass.ds(2 * b + u // 2, 1), :, HALF * (u % 2):HALF * (u % 2) + HALF].rearrange("a c n -> (a c) n"),
                                ot[u % 2][:, :]).then_inc(s_stored[u % 2], 16)
            program(e, norm, mlp)
            for v in (0, 1):
                e.wait_ge(s_stored[v], 16 * NIMG)

        @block.gpsimd
        def _(e):
            e.memset(centre[:, :], -1.0 / CH).then_inc(s_pz, 1)
            e.wait_ge(s_pz, 1)
            e.affine_select(out=centre[:, :], in_=centre[:, :], compare_op=ALU.not_equal, fill=1.0 - 1.0 / CH, base=0, pattern=[[-1, CH]], channel_multiplier=1).then_inc(s_pc, 1)

            def norm(b, p, early):
                for u in range(UNITS):
                    e.wait_ge(s_yn_hi, UNITS * b + u + 1)
                    if not early:
                        e.wait_ge(s_fc1, 3 * (UNITS * (b - 2) + u) + 3)
                    e.tensor_tensor(y16[1][:, p, u, :], yn[u % 2][:, :], y16[0][:, p, u, :], ALU.subtract).then_inc(s_yn_lo, 1)

            def mlp(b, p, early):
                for u in range(UNITS):
                    for m in range(3):
                        n = 3 * (UNITS * b + u) + m
                        e.wait_ge(s_g_hi, n + 1)
                        if not early or u >= 2:
                            e.wait_ge(s_fc2, UNITS * b + u - 1)
                        e.tensor_tensor(g16[1][:, 3 * (u % 2) + m, :], g32[m][:, :], g16[0][:, 3 * (u % 2) + m, :], ALU.subtract).then_inc(s_g_lo, 1)
            program(e, norm, mlp)

        @block.scalar
        def _(e):
            e.wait_ge(s_ready, 1)

            def norm(b, p, early):
                e.preload_act_table_set("natural_log_exp_and_others")
                for v in (0, 1):
                    i = 2 * p + v
                    e.wait_ge(s_h_loaded[i], 64 * (b - p) + 128)
                    if not (isinstance(b, int) and b == 0):
                        e.wait_ge(s_y, 2 * b + v - 1)
                    for y in (0, 1):
                        e.activation(hn[v][:, :].rearrange("c (r y k x) -> c y r k x", y=2, k=AC, x=PX)[:, y],
                                     ht[i][:, :, y, :, :].rearrange("c x r k -> c r k x"), ACT.Copy, scale=1.0 / H_SCALE).then_inc(s_hn, 1)
                for u in range(UNITS):
                    n = UNITS * b + u
                    e.wait_ge(s_centred, n + 1)
                    if not (isinstance(b, int) and b == 0 and u < 2):
                        e.wait_ge(s_var, n - 1)
                    e.activation(sqr[u % 2][:, :], PX_[u % 2][0:CH, :], ACT.Square).then_inc(s_sqr, 1)
                    e.wait_ge(s_var, n + 1)
                    if not (isinstance(b, int) and b == 0 and u < 1):
                        e.wait_ge(s_vy, n)
                    e.activation(vl[:, :], PV[u % 2][0:CH, :], ACT.Ln, bias=eps_c[:, :]).then_inc(s_vl, 1)
                    e.wait_ge(s_vl, n + 1)
                    if not (isinstance(b, int) and b == 0 and u < 2):
                        e.wait_ge(s_vr, n - 1)
                    e.activation(vy[u % 2][:, :], vl[:, :], ACT.Exp, scale=-0.5).then_inc(s_vy, 1)
                    if u >= 1:
                        high(b, p, u - 1, early)
                high(b, p, UNITS - 1, early)

            def high(b, p, u, early):
                e.wait_ge(s_yn, UNITS * b + u + 1)
                if not early:
                    e.wait_ge(s_fc1, 3 * (UNITS * (b - 2) + u) + 3)
                e.activation(y16[0][:, p, u, :], yn[u % 2][:, :], ACT.Copy).then_inc(s_yn_hi, 1)

            def mlp(b, p, early):
                for u in range(UNITS):
                    for m in range(3):
                        n = 3 * (UNITS * b + u) + m
                        e.wait_ge(s_fc1, n + 1)
                        if not early or u >= 1:
                            e.wait_ge(s_g_lo, n - 2)
                        e.activation(g32[m][:, :], PG[m][:, :], ACT.Gelu, bias=b1[:, m:m + 1]).then_inc(s_g, 1)
            program(e, norm, mlp)

        @block.vector
        def _(e):
            e.memset(mean_w[:, :], 1.0 / CH)
            e.memset(eps_c[:, :], 1e-5).then_inc(s_mw, 1)
            e.wait_ge(s_w_loaded, 16 * 8)
            e.tensor_scalar(w1g[:, :], w1r[:, :], g2c[:, :], None, ALU.mult).then_inc(s_wg, 1)
            e.wait_ge(s_wg, 1)
            e.tensor_copy(w1[0][:, :], w1g[:, :]).then_inc(s_wh, 1)
            e.tensor_copy(w2[0][:, :, :], w2r[:, :, :]).then_inc(s_wh, 1)
            e.wait_ge(s_wh, 2)
            e.tensor_tensor(w1[1][:, :], w1g[:, :], w1[0][:, :], ALU.subtract).then_inc(s_wl, 1)
            e.tensor_tensor(w2[1][:, :, :], w2r[:, :, :], w2[0][:, :, :], ALU.subtract).then_inc(s_wl, 1)
            e.wait_ge(s_bias, 1)
            e.tensor_tensor(b1[:, :], PO[:, 0:3], bf1c[:, :], ALU.add).then_inc(s_b1, 1)
            e.wait_ge(s_b1, 1); e.wait_ge(s_wl, 2); e.wait_ge(s_pc, 1); e.wait_ge(s_mw, 1)
            e.memset(va[:, :], 0.0).then_inc(s_ready, 1)
            e.wait_ge(s_ready, 1)

            def norm(b, p, early):
                for v in (0, 1):
                    i = 2 * p + v
                    e.wait_ge(s_hn, 4 * b + 2 * v + 2)
                    e.wait_ge(s_x_loaded[i], 8 * (b - p) + 16)
                    if not early:
                        e.wait_ge(s_out, UNITS * (b - 2) + 2 * v + 2)
                    e.tensor_tensor(yt[i][:, :], hn[v][:, :], xt[i][:, :], ALU.add).then_inc(s_y, 1)
                for u in range(UNITS):
                    n = UNITS * b + u
                    e.wait_ge(s_vy, n + 1)
                    e.scalar_tensor_tensor(va[:, :], PV[u % 2][0:CH, :], 1e-5, vy[u % 2][:, :], ALU.add, ALU.mult).then_inc(s_va, 1)
                    e.wait_ge(s_va, n + 1)
                    e.tensor_tensor(vb[:, :], va[:, :], vy[u % 2][:, :], ALU.mult).then_inc(s_vb, 1)
                    e.wait_ge(s_vb, n + 1)
                    e.scalar_tensor_tensor(vr[:, :], vb[:, :], 3.0, vy[u % 2][:, :], ALU.subtract, ALU.mult).then_inc(s_vr, 1)
                    e.wait_ge(s_vr, n + 1)
                    if not (isinstance(b, int) and b == 0 and u < 2):
                        e.wait_ge(s_yn_lo, n - 1)
                    e.scalar_tensor_tensor(yn[u % 2][:, :], PX_[u % 2][0:CH, :], -0.5, vr[:, :], ALU.mult, ALU.mult).then_inc(s_yn, 1)
                    e.wait_ge(s_yn, n + 1)

            def mlp(b, p, early):
                def result(u):
                    e.wait_ge(s_fc2, UNITS * b + u + 1)
                    if not early or u >= 2:
                        e.wait_ge(s_stored[u % 2], 16 * (2 * b + u // 2))
                    e.scalar_tensor_tensor(ot[u % 2][:, :], PO[0:CH, :], bf2c[:, :], yt[2 * p + u // 2][:, HALF * (u % 2):HALF * (u % 2) + HALF],
                                           ALU.add, ALU.add).then_inc(s_out, 1)
                for u in range(UNITS):
                    for m in range(3):
                        e.wait_ge(s_g, 3 * (UNITS * b + u) + m + 1)
                        if not early or u >= 2:
                            e.wait_ge(s_fc2, UNITS * b + u - 1)
                        e.tensor_copy(g16[0][:, 3 * (u % 2) + m, :], g32[m][:, :]).then_inc(s_g_hi, 1)
                    if u >= 1:
                        result(u - 1)
                result(UNITS - 1)
            program(e, norm, mlp)

        @block.tensor
        def _(e):
            e.wait_ge(s_w_loaded, 16 * 8)
            for m in range(3):
                mm = e.matmul(PO[:, m:m + 1], w1r[:, 128 * m:128 * m + 128], be2c[:, :], start=True, stop=True)
            mm.then_inc(s_bias, 1)
            e.wait_ge(s_ready, 1)
            PASSES = ((0, 0), (1, 0), (0, 1))

            def norm(b, p, early):
                def variance(u):
                    n = UNITS * b + u
                    e.wait_ge(s_sqr, n + 1)
                    if not (isinstance(b, int) and b == 0 and u < 2):
                        e.wait_ge(s_va, n - 1)
                    e.matmul(PV[u % 2][0:CH, :], mean_w[:, :], sqr[u % 2][:, :], start=True, stop=True).then_inc(s_var, 1)
                for u in range(UNITS):
                    n = UNITS * b + u
                    if u % 2 == 0:
                        e.wait_ge(s_y, 2 * b + u // 2 + 1)
                    if not (isinstance(b, int) and b == 0 and u < 2):
                        e.wait_ge(s_yn, n - 1)
                    e.matmul(PX_[u % 2][0:CH, :], centre[:, :], yt[2 * p + u // 2][:, HALF * (u % 2):HALF * (u % 2) + HALF], start=True, stop=True).then_inc(s_centred, 1)
                    if u >= 1: variance(u - 1)
                variance(UNITS - 1)

            def mlp(b, p, early):
                def down(u):
                    e.wait_ge(s_g_lo, 3 * (UNITS * b + u) + 3)
                    if not early or u >= 1:
                        e.wait_ge(s_out, UNITS * b + u)
                    for m in range(3):
                        for wp_, dp in PASSES:
                            mm = e.matmul(PO[0:CH, :], w2[wp_][:, m, :], g16[dp][:, 3 * (u % 2) + m, :], start=(m, wp_, dp) == (0, 0, 0), stop=(m, wp_, dp) == (2, 0, 1))
                    mm.then_inc(s_fc2, 1)
                for u in range(UNITS):
                    e.wait_ge(s_yn_lo, UNITS * b + u + 1)
                    for m in range(3):
                        n = 3 * (UNITS * b + u) + m
                        if not early or u >= 1:
                            e.wait_ge(s_g, n - 2)
                        for wp_, dp in PASSES:
                            mm = e.matmul(PG[m][:, :], w1[wp_][:, 128 * m:128 * m + 128], y16[dp][:, p, u, :], start=(wp_, dp) == (0, 0), stop=(wp_, dp) == (0, 1))
                        mm.then_inc(s_fc1, 1)
                    if u >= 1: down(u - 1)
                down(UNITS - 1)
            program(e, norm, mlp)

_INS = ['x'] + ['L0_conv_' + n for n in ('wq', 'sq', 'bq', 'wkv', 'skv', 'bkv', 'wp', 'sp', 'bp', 'w1', 's1', 'b1', 'wdw', 'bdw', 'w2', 's2', 'b2')] \
    + ['L1_conv_' + n for n in ('g1', 'b1', 'Wc', 'g2', 'b2', 'w_fc1', 'b_fc1', 'w_fc2', 'b_fc2')]


def build(nc, x, wq, sq, bq, wkv, skv, bkv, wp, sp, bp, w1, s1, b1, wdw, bdw, w2, s2, b2, g1, be1, Wc, g2, be2, wf1, bf1, wf2, bf2, out):
    x2 = nc.dram_tensor("x2_scratch", (NIMG, CH, PIX), F32, kind="Internal").ap()
    xn = nc.dram_tensor("xn_scratch", (NIMG, GROUPS, 128, NB_B), F32, kind="Internal").ap()
    h = nc.dram_tensor("h_scratch", (NIMG, GROUPS, 128, NB_A), F32, kind="Internal").ap()
    attention_block(nc, x.rearrange("b c h w -> b c (h w)"), wq, sq, bq, wkv, skv, bkv, wp, sp, bp, w1, s1, b1, wdw, bdw, w2, s2, b2, g1, be1, x2, xn)
    nnmf(nc, Wc, xn, h)
    token_mlp(nc, x2, h, g2, be2, wf1, bf1, wf2, bf2, out.rearrange("b c h w -> b c (h w)"))


def kernel(**inputs):
    import concourse.bacc as bacc
    from concourse.bass_utils import run_bass_kernel_spmd

    nc = bacc.Bacc("TRN2", target_bir_lowering=False, num_devices=1)
    arrays, args = {}, []
    for name in _INS:
        a = np.ascontiguousarray(inputs[name])
        arrays["in_" + name] = a
        args.append(nc.dram_tensor("in_" + name, a.shape, mybir.dt.from_np(a.dtype), kind="ExternalInput").ap())
    out = nc.dram_tensor("out", (NIMG, CH, HW, HW), F32, kind="ExternalOutput").ap()
    build(nc, *args, out)
    r = run_bass_kernel_spmd(nc, [arrays], core_ids=[0])
    return r.results[0]["out"]
```
